# Optimizing a Trainium2 kernel written in Bass

```python
import numpy as np
import jax
import jax.numpy as jnp

def _softmax(x, axis=-1):
    return jax.nn.softmax(x, axis=axis)

def _gelu(x):
    return jax.nn.gelu(x, approximate=True)

def _silu(x):
    return jax.nn.silu(x)

def _sigmoid(x):
    return jax.nn.sigmoid(x)

def _layernorm(x, axis=-1, eps=1e-05):
    m = jnp.mean(x, axis=axis, keepdims=True)
    v = jnp.var(x, axis=axis, keepdims=True)
    return (x - m) / jnp.sqrt(v + eps)

def _scatter_add(tgt, idx, src, axis=0):
    return tgt.at[idx].add(src)

def _segment_sum(src, seg, n):
    return jax.ops.segment_sum(src, seg, n)
kernel_name = 'mk_adj_preln_d2_adj_r2_5ba231'

def setup_inputs(seed: int=0):
    np.random.seed(seed)
    _w = jnp.asarray

    def _rec_inputs():
        import jax
        import jax.numpy as jnp
        _gk = jax.random.key(seed)
        x = -0.0002928 + 1 * jax.random.normal(jax.random.fold_in(_gk, 1), (8, 1024, 256), jnp.float32)
        _a = jax.random.bernoulli(jax.random.fold_in(_gk, 2), 0.00195312, (1024, 1024))
        _a = jnp.logical_or(_a, jnp.swapaxes(_a, -1, -2))
        _a = jnp.logical_or(_a, jnp.eye(1024, dtype=bool))
        adj = _a.astype(jnp.int32)
        return (x, adj)
    x, adj = _rec_inputs()

    def _L0_gnn_setup():
        import jax, jax.numpy as jnp
        import numpy as np
        D_MODEL = 256
        NUM_HEADS = 8
        D_HEAD = D_MODEL // NUM_HEADS
        B, N = (4, 1024)
        key = jax.random.key(seed)
        ks = jax.random.split(key, 10)
        s = 1.0 / np.sqrt(D_MODEL)
        inp = {'h': jax.random.normal(ks[0], (B, N, D_MODEL), dtype=jnp.float32), 'adj': jax.random.randint(ks[1], (N, N), 0, 2, dtype=jnp.int32), 'Wq': jax.random.uniform(ks[2], (D_MODEL, D_MODEL), jnp.float32, -s, s), 'bq': jax.random.uniform(ks[3], (D_MODEL,), jnp.float32, -s, s), 'Wk': jax.random.uniform(ks[4], (D_MODEL, D_MODEL), jnp.float32, -s, s), 'bk': jax.random.uniform(ks[5], (D_MODEL,), jnp.float32, -s, s), 'Wv': jax.random.uniform(ks[6], (D_MODEL, D_MODEL), jnp.float32, -s, s), 'bv': jax.random.uniform(ks[7], (D_MODEL,), jnp.float32, -s, s), 'Wo': jax.random.uniform(ks[8], (D_MODEL, D_MODEL), jnp.float32, -s, s), 'bo': jax.random.uniform(ks[9], (D_MODEL,), jnp.float32, -s, s)}
        return inp
    _L0_gnn_all = _L0_gnn_setup()
    _L0_gnn_in = {k: v for k, v in _L0_gnn_all.items() if k in ('Wq', 'bq', 'Wk', 'bk', 'Wv', 'bv', 'Wo', 'bo')}
    del _L0_gnn_all

    def _L1_gnn_setup():
        import jax, jax.numpy as jnp
        import numpy as np
        B, K, DIN, DOUT = (32, 64, 256, 256)
        key = jax.random.key(seed)
        k1, k2, k3, k4 = jax.random.split(key, 4)
        x = jax.random.normal(k1, (B, K, DIN), dtype=jnp.float32)
        adj = jax.random.randint(k2, (K, K), 0, 2, dtype=jnp.int32)
        W = jax.random.normal(k3, (DOUT, 2 * DIN), dtype=jnp.float32) * 0.02
        b = jax.random.normal(k4, (DOUT,), dtype=jnp.float32) * 0.02
        return {'x': x, 'adj': adj, 'W': W, 'b': b}
    _L1_gnn_all = _L1_gnn_setup()
    _L1_gnn_in = {k: v for k, v in _L1_gnn_all.items() if k in ('W', 'b')}
    del _L1_gnn_all
    return {'x': x, 'adj': adj, 'L0_gnn_Wq': _L0_gnn_in['Wq'], 'L0_gnn_bq': _L0_gnn_in['bq'], 'L0_gnn_Wk': _L0_gnn_in['Wk'], 'L0_gnn_bk': _L0_gnn_in['bk'], 'L0_gnn_Wv': _L0_gnn_in['Wv'], 'L0_gnn_bv': _L0_gnn_in['bv'], 'L0_gnn_Wo': _L0_gnn_in['Wo'], 'L0_gnn_bo': _L0_gnn_in['bo'], 'L1_gnn_W': _L1_gnn_in['W'], 'L1_gnn_b': _L1_gnn_in['b']}

def reference(x, adj, L0_gnn_Wq, L0_gnn_bq, L0_gnn_Wk, L0_gnn_bk, L0_gnn_Wv, L0_gnn_bv, L0_gnn_Wo, L0_gnn_bo, L1_gnn_W, L1_gnn_b):
    import jax
    import jax.numpy as jnp

    def _L0_gnn_ref(h, adj, Wq, bq, Wk, bk, Wv, bv, Wo, bo):
        import jax, jax.numpy as jnp
        import numpy as np
        D_MODEL = 256
        NUM_HEADS = 8
        D_HEAD = D_MODEL // NUM_HEADS
        B, N = (4, 1024)
        b, n, _ = h.shape

        def split_heads(x):
            return x.reshape(b, n, NUM_HEADS, D_HEAD).transpose(0, 2, 1, 3)
        q = split_heads(h @ Wq.T + bq)
        k = split_heads(h @ Wk.T + bk)
        v = split_heads(h @ Wv.T + bv)
        scale = 1.0 / np.sqrt(D_HEAD)
        scores = jnp.einsum('bhqd,bhkd->bhqk', q, k) * scale
        mask = (adj == 0)[None, None, :, :]
        scores = jnp.where(mask, -jnp.inf, scores)
        attn = jax.nn.softmax(scores, axis=-1)
        out = jnp.einsum('bhqk,bhkd->bhqd', attn, v)
        out = out.transpose(0, 2, 1, 3).reshape(b, n, D_MODEL)
        return out @ Wo.T + bo

    def _L1_gnn_ref(x, adj, W, b):
        import jax, jax.numpy as jnp
        import numpy as np
        B, K, DIN, DOUT = (32, 64, 256, 256)
        Din = x.shape[-1]
        Wi, Wj = (W[:, :Din], W[:, Din:])
        mi = jnp.einsum('bkd,od->bko', x, Wi)
        mj = jnp.einsum('bkd,od->bko', x, Wj)
        a = adj.astype(x.dtype)
        deg = a.sum(axis=1)
        out = deg[None, :, None] * (mi + b) + jnp.einsum('ij,bjo->bio', a, mj)
        return out
    h = jnp.maximum(_layernorm(x, axis=-1), 0.0)
    x = x + _L0_gnn_ref(h, adj, L0_gnn_Wq, L0_gnn_bq, L0_gnn_Wk, L0_gnn_bk, L0_gnn_Wv, L0_gnn_bv, L0_gnn_Wo, L0_gnn_bo)
    h = jnp.maximum(_layernorm(x, axis=-1), 0.0)
    x = x + _L1_gnn_ref(h, adj, L1_gnn_W, L1_gnn_b)
    return x

_drawn_inputs = setup_inputs


def setup_inputs(seed=0):
    import zlib

    import numpy as np

    out = dict(_drawn_inputs(seed))
    spreads = {}
    factors = {'L0_gnn_Wq': 5.952,
     'L0_gnn_bq': 8.0,
     'L0_gnn_Wk': 5.825,
     'L0_gnn_bk': 8.0,
     'L0_gnn_bv': 2.727}
    for name, (base, spread) in spreads.items():
        noise = np.random.default_rng([zlib.crc32(name.encode()), seed]).standard_normal(out[name].shape)
        drawn = base * np.exp(spread * noise) if base else spread * noise
        out[name] = jnp.asarray(drawn.astype(out[name].dtype))
    for name, factor in factors.items():
        out[name] = (out[name] * factor).astype(out[name].dtype)
    return out
```

```python
from contextlib import ExitStack

import concourse.bass as bass
from concourse import mybir

F32 = mybir.dt.float32
F16 = mybir.dt.float16
BF16 = mybir.dt.bfloat16
I32 = mybir.dt.int32
ALU = mybir.AluOpType
ACT = mybir.ActivationFunctionType
AX_X = mybir.AxisListType.X

B, N, D = 8, 1024, 256
HEADS, DH = 8, 32
P = 128
NT = N // P
KC = D // P
GH = P // DH
QB = 4
UNITS = HEADS * NT
BLOCKS = UNITS // 8
W_SCALE = 64.0
SCALE = float(DH) ** -0.5
EPS = 1e-5
NEG = -1e30
WQ, WK, WV, WO, WI = 0, D, 2 * D, 3 * D, 4 * D
W_COLS = 6 * D
TERMS = [(0, 0), (0, 1), (1, 0)]


def unit(u):
    return u // 32, (u // 8) % QB, (u // 2) % GH, u % 2


def gnn_kernel(nc, x, adj, w_t, b_qk, b_v, b_o, b_msg, ident, out):
    with ExitStack() as ctx:
        def sb(name, shape, dt):
            return ctx.enter_context(nc.sbuf_tensor(name, shape, dt))

        def pb(name, shape, dt):
            return ctx.enter_context(nc.psum_tensor(name, shape, dt))

        ident32 = sb("ident32", [P, P], F32)
        ident16 = sb("ident16", [P, P], F16)
        w16 = sb("w16", [P, 2, KC, W_COLS], F16)
        bias_qk = sb("bias_qk", [P, 2, KC], F32)
        bias_v = sb("bias_v", [P, D], F32)
        bias_o = sb("bias_o", [P, D], F32)
        bias_msg = sb("bias_msg", [P, D], F32)
        minus_half = sb("minus_half", [P, 2], F32)
        mask_add = sb("mask_add", [P, NT, N], BF16)
        adj_t = sb("adj_t", [P, NT, N], F16)
        deg = sb("deg", [P, NT], F32)
        q_op = sb("q_op", [P, HEADS, N], F16)
        k_op = sb("k_op", [P, HEADS, N], F16)
        v_op = sb("v_op", [P, KC, NT, P], F32)
        qk_next = sb("qk_next", [P, 2, 2, KC, N], F16)
        v_next = sb("v_next", [P, NT, D], F32)
        probs = sb("probs", [P, 3, N], F32)
        probs_t = sb("probs_t", [P, GH, NT, 2 * P], F32)
        neg_max = sb("neg_max", [P, UNITS], F32)
        row_sum = sb("row_sum", [P, UNITS], F32)
        inv_sum = sb("inv_sum", [P, 2, GH, DH], F32)
        inv_sum_t = sb("inv_sum_t", [P, 2 * P], F32)
        o32 = sb("o32", [P, 2 * P], F32)
        o16 = sb("o16", [P, 2, KC, N], F16)
        x_in = sb("x_in", [P, 2, 2, D], F32)
        x1 = sb("x1", [P, 2, D], F32)
        stats = sb("stats", [P, 16, 6], F32)
        mean_var = sb("mean_var", [P, 16, 2], F32)
        var_eps = sb("var_eps", [P, 16], F32)
        rstd = sb("rstd", [P, 16], F32)
        neg_mean = sb("neg_mean", [P, 16], F32)
        h32 = sb("h32", [P, 2, D], F32)
        h16 = sb("h16", [P, 2, 2, D], F16)
        h_t = sb("h_t", [P, 2, KC, 2 * P], F16)
        qk32 = sb("qk32", [P, 2, KC, 2 * P], F32)
        msg16 = sb("msg16", [P, NT, 2, D], F16)
        self32 = sb("self32", [P, D], F32)
        base = sb("base", [P, NT, D], F32)
        out32 = sb("out32", [P, 2, 2, D], F32)

        adj_raw = probs_t[:, :, :, :].bitcast(I32).rearrange("p h k q -> p (h k q)").rearrange("p (t n) -> p t n", t=NT)
        adj16 = qk32[:, :, :, :].bitcast(F16).rearrange("p a b n -> p (a b n)").rearrange("p (t n) -> p t n", t=2)
        w_raw = probs[:, :, :].rearrange("p a n -> p (a n)").rearrange("p (c n) -> p c n", c=KC)

        s_ps = pb("s_ps", [P, 2, N], F32)
        t_ps = pb("t_ps", [P, 2, 512], F32)
        o_ps = pb("o_ps", [P, 512], F32)
        side_ps = pb("side_ps", [P, 512], F32)

        sems = {}

        def sem(name):
            sems[name] = ctx.enter_context(nc.semaphore(name))
            return sems[name]

        s_const = sem("s_const")
        s_wload = sem("s_wload")
        s_adjload = [sem(f"s_adjload{t}") for t in range(NT)]
        s_id16 = sem("s_id16")
        s_half = sem("s_half")
        s_whi = sem("s_whi")
        s_wlo = sem("s_wlo")
        s_adj16 = sem("s_adj16")
        s_mask = sem("s_mask")
        s_adjtp = sem("s_adjtp")
        s_adjt = sem("s_adjt")
        s_scores = sem("s_scores")
        s_masked = sem("s_masked")
        s_exp = sem("s_exp")
        s_tp = sem("s_tp")
        s_copy0 = sem("s_copy0")
        s_copy1 = sem("s_copy1")
        s_pv = sem("s_pv")
        s_inv = sem("s_inv")
        s_invtp = sem("s_invtp")
        s_invt = sem("s_invt")
        s_o32 = sem("s_o32")
        s_ohi = sem("s_ohi")
        s_olo = sem("s_olo")
        s_x = [sem("s_x0"), sem("s_x1")]
        s_stats = sem("s_stats")
        s_moments = sem("s_moments")
        s_vareps = sem("s_vareps")
        s_rstd = sem("s_rstd")
        s_negmean = sem("s_negmean")
        s_relu = sem("s_relu")
        s_hhi = sem("s_hhi")
        s_hlo = sem("s_hlo")
        s_side = sem("s_side")
        s_ht = sem("s_ht")
        s_qk32 = sem("s_qk32")
        s_qkhi = sem("s_qkhi")
        s_qklo = sem("s_qklo")
        s_v = sem("s_v")
        s_xbias = sem("s_xbias")
        s_x1done = sem("s_x1done")
        s_msghi = sem("s_msghi")
        s_msglo = sem("s_msglo")
        s_self = sem("s_self")
        s_base = sem("s_base")
        s_sums = sem("s_sums")
        s_out = sem("s_out")
        s_stored = [sem("s_stored0"), sem("s_stored1")]
        s_op0 = sem("s_op0")
        s_op1 = sem("s_op1")
        data_sems = dict(sems)
        s_arrive = sem("s_arrive")
        go = {e: sem(f"s_go_{e}") for e in ("pe", "act", "dve", "sp")}

        OP_DMAS = 2 * GH * 4 + 1
        x_t = x.rearrange("b (t p) c -> b p t c", p=P)
        out_t = out.rearrange("b (t p) c -> b p t c", p=P)


        FRONT_TOTALS = {
            "s_x0": 32, "s_x1": 32, "s_stats": 8, "s_moments": 8, "s_vareps": 4, "s_rstd": 4, "s_negmean": 4,
            "s_relu": 4, "s_hhi": 4, "s_hlo": 4, "s_side": 16, "s_ht": 4, "s_qk32": 8,
            "s_qkhi": 8, "s_qklo": 8, "s_v": 4, "s_op0": 16 * OP_DMAS,
        }
        SETUP_TOTALS = FRONT_TOTALS | {
            "s_const": 16 * 5, "s_wload": 16, "s_id16": 2, "s_half": 1, "s_whi": 1, "s_wlo": 1, "s_adj16": NT,
            "s_mask": NT, "s_adjtp": NT, "s_adjt": NT,
        } | {f"s_adjload{t}": 16 for t in range(NT)}
        ROUND_TOTALS = FRONT_TOTALS | {
            "s_scores": UNITS, "s_masked": UNITS, "s_exp": UNITS, "s_tp": 2 * UNITS, "s_copy0": UNITS,
            "s_copy1": UNITS, "s_pv": BLOCKS, "s_inv": BLOCKS, "s_invtp": BLOCKS, "s_invt": BLOCKS,
            "s_o32": BLOCKS, "s_ohi": BLOCKS, "s_olo": BLOCKS,
            "s_x0": 64, "s_x1": 64, "s_stats": 16, "s_moments": 16, "s_vareps": 8, "s_rstd": 8, "s_negmean": 8,
            "s_relu": 8, "s_hhi": 8, "s_hlo": 8, "s_side": 32, "s_ht": 8,
            "s_xbias": 4, "s_x1done": 4, "s_msghi": 8, "s_msglo": 8, "s_self": 8, "s_base": 8,
            "s_sums": 4, "s_out": 4, "s_stored0": 32, "s_stored1": 32, "s_op1": 16 * OP_DMAS,
        }

        STEPS = UNITS + 13

        def pv_step(k):
            return 8 * k + 10

        def front_pair(s, offset):
            n, o = divmod(s - offset, 8)
            return n if o == 0 and 0 <= n < 4 else None

        def tail_pair(s, offset):
            j, o = divmod(s - offset - pv_step(QB), 8)
            return j if o == 0 and 0 <= j < 4 else None

        def block_at(s, offset):
            k, o = divmod(s - offset - 10, 8)
            return k if o == 0 and 0 <= k < BLOCKS else None

        def leave_round(eng, name):
            eng.sem_inc(s_arrive, 1)
            eng.wait_ge(go[name], 1)
            eng.sem_clear(go[name])

        block = ctx.enter_context(nc.Block())

        @block.sync
        def _(sp):
            def load_front(n, b_next):
                if n >= 2:
                    sp.wait_ge(s_relu, n - 1)
                sp.dma_start(x_in[:, n % 2, :, :], x_pair(b_next, n)).then_inc(s_x[n % 2], 16)

            def x_pair(b, n):
                return x_t[bass.ds(b, 1), :, 2 * n:2 * n + 2, :].rearrange("b p t c -> p (b t) c")

            def load_tail(j, b):
                n = QB + j
                if j < 2:
                    sp.wait_ge(s_relu, n - 1)
                else:
                    sp.wait_ge(s_x1done, j - 1)
                sp.dma_start(x_in[:, n % 2, :, :], x_pair(b, j)).then_inc(s_x[n % 2], 16)

            def move_operands(g, done):
                for h in range(GH):
                    rows = slice(DH * h, DH * h + DH)
                    for r, (q_part, k_part) in enumerate([(0, 0), (0, 1), (1, 0), (1, 1)]):
                        to = slice(DH * r, DH * r + DH)
                        sp.dma_start(q_op[to, GH * g + h, :], qk_next[rows, 0, q_part, g, :]).then_inc(done, 16)
                        sp.dma_start(k_op[to, GH * g + h, :], qk_next[rows, 1, k_part, g, :]).then_inc(done, 16)
                sp.dma_start(v_op[:, g, :, :], v_next[:, :, P * g:P * g + P]).then_inc(done, 16)

            def move_group0():
                sp.wait_ge(s_qkhi, 8)
                sp.wait_ge(s_qklo, 8)
                sp.wait_ge(s_v, 4)
                move_operands(0, s_op0)

            sp.dma_start(w_raw, w_t.rearrange("(c p) n -> p c n", p=P)).then_inc(s_wload, 16)
            sp.dma_start(ident32[:, :], ident).then_inc(s_const, 16)
            sp.dma_start(bias_qk[:, :, :], b_qk).then_inc(s_const, 16)
            for to, of in ((bias_v, b_v), (bias_o, b_o), (bias_msg, b_msg)):
                sp.dma_start(to[:, :], of.to_broadcast([P, D])).then_inc(s_const, 16)
            load_front(0, 0)
            load_front(1, 0)
            for t in range(NT):
                sp.dma_start(adj_raw[:, t, :], adj[P * t:P * t + P, :]).then_inc(s_adjload[t], 16)
            load_front(2, 0)
            load_front(3, 0)
            move_group0()
            leave_round(sp, "sp")

            with sp.Fori(0, B) as b:
                b_next = (b + 1) % B
                move_operands(1, s_op1)
                for n in range(4):
                    load_front(n, b_next)
                load_tail(0, b)
                load_tail(1, b)
                sp.wait_ge(s_scores, UNITS // 2)
                sp.wait_ge(s_pv, QB)
                move_group0()
                load_tail(2, b)
                load_tail(3, b)
                for i in range(NT // 2):
                    sp.wait_ge(s_out, i + 1)
                    sp.dma_start(out_t[bass.ds(b, 1), :, 2 * i:2 * i + 2, :].rearrange("b p t c -> p (b t) c"),
                                 out32[:, i % 2, :, :]).then_inc(s_stored[i % 2], 16)
                leave_round(sp, "sp")

        @block.tensor
        def _(pe):
            def adj_transposes(t):
                pe.wait_ge(s_adj16, t + 1)
                if t >= 2:
                    pe.wait_ge(s_adjt, t - 1)
                bank = t_ps[:, t % 2, :].bitcast(F16)
                for j in range(NT):
                    mm = pe.transpose(bank[:, P * j:P * j + P], adj16[:, t % 2, P * j:P * j + P], ident16[:, :])
                mm.then_inc(s_adjtp, 1)

            def scores(u):
                g, qb, hh, qt = unit(u)
                if u >= 2:
                    pe.wait_ge(s_masked, u - 1)
                if u == UNITS // 2:
                    pe.wait_ge(s_op1, 16 * OP_DMAS)
                h = GH * g + hh
                at = (2 * qb + qt) * P
                for c in range(2):
                    mm = pe.matmul(s_ps[:, u % 2, 512 * c:512 * c + 512], q_op[:, h, at:at + P],
                                   k_op[:, h, 512 * c:512 * c + 512], start=True, stop=True)
                mm.then_inc(s_scores, 1)

            def transposes(u):
                pe.wait_ge(s_exp, u + 1)
                for half in range(2):
                    if u >= 1:
                        pe.wait_ge((s_copy0, s_copy1)[half], u)
                    for j in range(4):
                        k = 4 * half + j
                        mm = pe.transpose(t_ps[:, half, P * j:P * j + P], probs[:, u % 3, P * k:P * k + P],
                                          ident32[:, :])
                    mm.then_inc(s_tp, 1)

            def times_v(k):
                g = k // QB
                pe.wait_ge(s_copy0, 8 * k + 8)
                pe.wait_ge(s_copy1, 8 * k + 8)
                if k >= 1:
                    pe.wait_ge(s_o32, k)
                for t in range(NT):
                    for hh in range(GH):
                        at = slice(DH * hh, DH * hh + DH)
                        mm = pe.matmul(o_ps[at, 0:2 * P], v_op[:, g, t, at], probs_t[:, hh, t, :],
                                       start=(t == 0), stop=(t == NT - 1))
                mm.then_inc(s_pv, 1)
                pe.wait_ge(s_inv, k + 1)
                for qt in range(2):
                    mm = pe.transpose(o_ps[:, 2 * P + P * qt:2 * P + P * qt + P],
                                      inv_sum[:, qt, :, :].rearrange("p h d -> p (h d)"), ident32[:, :])
                mm.then_inc(s_invtp, 1)

            def turn_h(n):
                pe.wait_ge(s_hhi, n + 1)
                pe.wait_ge(s_hlo, n + 1)
                if n >= 4:
                    pe.wait_ge(s_x1done, n - 3)
                elif n >= 1:
                    pe.wait_ge(s_v, n)
                bank = side_ps[:, :].bitcast(F16).rearrange("p (a c n) -> p a c n", a=2, c=KC)
                for part in range(2):
                    for c in range(KC):
                        for t in range(2):
                            mm = pe.transpose(bank[:, part, c, P * t:P * t + P], h16[:, part, t, P * c:P * c + P],
                                              ident16[:, :])
                mm.then_inc(s_side, 1)

            def q_or_k(n, which):
                if which == 0:
                    pe.wait_ge(s_ht, n + 1)
                else:
                    pe.wait_ge(s_qk32, 2 * n + 1)
                for g in range(KC):
                    col = (WQ, WK)[which] + P * g
                    for i, (w_part, h_part) in enumerate(TERMS):
                        for c in range(KC):
                            mm = pe.matmul(side_ps[:, 2 * P * g:2 * P * g + 2 * P], w16[:, w_part, c, col:col + P],
                                           h_t[:, h_part, c, :], start=(i + c == 0), stop=(i == 2 and c == KC - 1))
                mm.then_inc(s_side, 1)

            def v_pair(n):
                pe.wait_ge(s_qk32, 2 * n + 2)
                for t in range(2):
                    for i, (h_part, w_part) in enumerate(TERMS):
                        for c in range(KC):
                            mm = pe.matmul(side_ps[:, D * t:D * t + D], h_t[:, h_part, c, P * t:P * t + P],
                                           w16[:, w_part, c, WV:WV + D], start=(i + c == 0),
                                           stop=(i == 2 and c == KC - 1))
                mm.then_inc(s_side, 1)

            def messages_read(tiles):
                pe.wait_ge(s_msghi, tiles)
                pe.wait_ge(s_msglo, tiles)

            def output_product(j):
                pe.wait_ge(s_ohi, QB + j + 1)
                pe.wait_ge(s_olo, QB + j + 1)
                if j == 0:
                    pe.wait_ge(s_v, 4)
                else:
                    messages_read(2 * j)
                for t in range(2):
                    at = (2 * j + t) * P
                    for i, (o_part, w_part) in enumerate(TERMS):
                        for c in range(KC):
                            mm = pe.matmul(side_ps[:, D * t:D * t + D], o16[:, o_part, c, at:at + P],
                                           w16[:, w_part, c, WO:WO + D], start=(i + c == 0),
                                           stop=(i == 2 and c == KC - 1))
                mm.then_inc(s_side, 1)

            def messages(j, t):
                if t == 0:
                    pe.wait_ge(s_ht, 4 + j + 1)
                else:
                    messages_read(2 * j + 1)
                for i, (h_part, w_part) in enumerate(TERMS):
                    for c in range(KC):
                        mm = pe.matmul(side_ps[:, :], h_t[:, h_part, c, P * t:P * t + P],
                                       w16[:, w_part, c, WI:WI + 2 * D], start=(i + c == 0),
                                       stop=(i == 2 and c == KC - 1))
                mm.then_inc(s_side, 1)

            def neighbour_sums(j_tiles):
                pe.wait_ge(s_msghi, j_tiles[-1] + 1)
                pe.wait_ge(s_msglo, j_tiles[-1] + 1)
                if j_tiles[0] == 0:
                    pe.wait_ge(s_masked, UNITS)
                for i in range(NT):
                    for j in j_tiles:
                        for part in range(2):
                            mm = pe.matmul(s_ps[:, i // 4, D * (i % 4):D * (i % 4) + D], adj_t[:, j, P * i:P * i + P],
                                           msg16[:, j, part, :], start=(j == 0 and part == 0 and i % 2 == 0),
                                           stop=(j == NT - 1 and part == 1), skip_group_check=True)
                    if j_tiles[-1] == NT - 1 and i % 2 == 1:
                        mm.then_inc(s_sums, 1)

            def front(s):
                if (n := front_pair(s, 4)) is not None:
                    turn_h(n)
                if (n := front_pair(s, 5)) is not None:
                    q_or_k(n, 0)
                if (n := front_pair(s, 6)) is not None:
                    q_or_k(n, 1)
                if (n := front_pair(s, 7)) is not None:
                    v_pair(n)

            pe.wait_ge(s_id16, 2)
            pe.wait_ge(s_whi, 1)
            pe.wait_ge(s_wlo, 1)
            for s in range(32):
                front(s)
            for t in range(NT):
                adj_transposes(t)
            leave_round(pe, "pe")

            with pe.Fori(0, B):
                for s in range(STEPS):
                    if s < UNITS:
                        scores(s)
                    if (k := block_at(s, 0)) is not None:
                        times_v(k)
                    if 0 <= s - 2 < UNITS:
                        transposes(s - 2)
                    front(s)
                    if (j := tail_pair(s, 3)) is not None:
                        output_product(j)
                    if (j := tail_pair(s, 6)) is not None:
                        turn_h(4 + j)
                    if (j := tail_pair(s, 7)) is not None:
                        messages(j, 0)
                    if (j := tail_pair(s, 8)) is not None:
                        messages(j, 1)
                    if s == UNITS + 6:
                        neighbour_sums(range(0, 6))
                neighbour_sums(range(6, 8))
                leave_round(pe, "pe")

        @block.scalar
        def _(act):
            def exponentials(u):
                act.wait_ge(s_masked, u + 1)
                nc.scalar.activation(probs[:, u % 3, :], probs[:, u % 3, :], ACT.Exp, bias=neg_max[:, u:u + 1],
                                     scale=-1.0, accum_out=row_sum[:, u:u + 1]).then_inc(s_exp, 1)

            def copy_half(u):
                _, _, hh, qt = unit(u)
                act.wait_ge(s_tp, 2 * u + 1)
                nc.scalar.copy(probs_t[:, hh, 0:4, P * qt:P * qt + P],
                               t_ps[:, 0, :].rearrange("p (k q) -> p k q", k=4)).then_inc(s_copy0, 1)

            def copy_inverse(k):
                act.wait_ge(s_invtp, k + 1)
                if k >= 1:
                    act.wait_ge(s_o32, k)
                nc.scalar.copy(inv_sum_t[:, :], o_ps[:, 2 * P:4 * P]).then_inc(s_invt, 1)

            def relu(n):
                act.wait_ge(s_negmean, n + 1)
                if n >= 1:
                    act.wait_ge(s_hhi, n)
                    act.wait_ge(s_hlo, n)
                source = x_in[:, n % 2, :, :] if n < 4 else x1[:, :, :]
                for t in range(2):
                    i = 2 * n + t
                    op = nc.scalar.activation(h32[:, t, :], source[:, t, :], ACT.Relu, bias=neg_mean[:, i:i + 1],
                                              scale=rstd[:, i:i + 1])
                op.then_inc(s_relu, 1)

            def copy_h_t(n):
                i = 4 * n if n < 4 else 4 * n + 1
                act.wait_ge(s_side, i + 1)
                nc.scalar.copy(h_t[:, :, :, :].rearrange("p a c n -> p (a c n)"),
                               side_ps[:, :].bitcast(F16)).then_inc(s_ht, 1)

            def evict_qk(n, which):
                act.wait_ge(s_side, 4 * n + 2 + which)
                if n >= 1:
                    act.wait_ge(s_qkhi, 2 * n - 1 + which)
                    act.wait_ge(s_qklo, 2 * n - 1 + which)
                for g in range(KC):
                    op = nc.scalar.activation(qk32[:, which, g, :], side_ps[:, 2 * P * g:2 * P * g + 2 * P],
                                              ACT.Identity, bias=bias_qk[:, which, g:g + 1],
                                              scale=(SCALE if which == 0 else 1.0) / W_SCALE)
                op.then_inc(s_qk32, 1)

            def message_hi(j, t):
                act.wait_ge(s_side, 16 + 4 * j + 3 + t)
                nc.scalar.copy(msg16[:, 2 * j + t, 0, :], side_ps[:, D:2 * D]).then_inc(s_msghi, 1)

            def front(s):
                if (n := front_pair(s, 2)) is not None:
                    relu(n)
                if (n := front_pair(s, 4)) is not None:
                    copy_h_t(n)
                if (n := front_pair(s, 5)) is not None:
                    evict_qk(n, 0)
                if (n := front_pair(s, 6)) is not None:
                    evict_qk(n, 1)

            act.wait_ge(s_wload, 16)
            nc.scalar.activation(w16[:, 0, :, :], w_raw, ACT.Copy, scale=W_SCALE).then_inc(s_whi, 1)
            act.wait_ge(s_id16, 2)
            for s in range(32):
                front(s)
            for t in range(NT):
                act.wait_ge(s_adjload[t], 16)
                if t == 0:
                    act.wait_ge(s_qklo, 8)
                    act.wait_ge(s_qkhi, 8)
                if t >= 2:
                    act.wait_ge(s_adjtp, t - 1)
                nc.scalar.activation(adj16[:, t % 2, :], adj_raw[:, t, :], ACT.Copy,
                                     accum_out=deg[:, t:t + 1]).then_inc(s_adj16, 1)
            leave_round(act, "act")

            with act.Fori(0, B):
                for s in range(STEPS):
                    if 0 <= s - 2 < UNITS:
                        copy_half(s - 2)
                    if (k := block_at(s, 0)) is not None:
                        copy_inverse(k)
                    if s < UNITS:
                        exponentials(s)
                    front(s)
                    if (j := tail_pair(s, 4)) is not None:
                        relu(4 + j)
                    if (j := tail_pair(s, 6)) is not None:
                        copy_h_t(4 + j)
                    if (j := tail_pair(s, 7)) is not None:
                        message_hi(j, 0)
                    if (j := tail_pair(s, 8)) is not None:
                        message_hi(j, 1)
                leave_round(act, "act")

        @block.vector
        def _(dve):
            def mask_scores(u):
                _, qb, _, qt = unit(u)
                dve.wait_ge(s_scores, u + 1)
                if u >= 3:
                    dve.wait_ge(s_tp, 2 * (u - 3) + 2)
                nc.vector.tensor_tensor_reduce(
                    out=probs[:, u % 3, :], in0=s_ps[:, u % 2, :], in1=mask_add[:, 2 * qb + qt, :], scale=-1.0,
                    scalar=3e38, op0=ALU.add, op1=ALU.min, accum_out=neg_max[:, u:u + 1]).then_inc(s_masked, 1)

            def copy_half(u):
                _, _, hh, qt = unit(u)
                dve.wait_ge(s_tp, 2 * u + 2)
                nc.vector.tensor_copy(probs_t[:, hh, 4:8, P * qt:P * qt + P],
                                      t_ps[:, 1, :].rearrange("p (k q) -> p k q", k=4)).then_inc(s_copy1, 1)

            def inverse_sums(k):
                dve.wait_ge(s_exp, 8 * k + 8)
                if k >= 1:
                    dve.wait_ge(s_invtp, k)
                sums = row_sum[:, 8 * k:8 * k + 8].rearrange("p (h q) -> p q h", q=2)
                nc.vector.reciprocal(inv_sum[:, :, :, :],
                                     sums[:, :, :, None].to_broadcast([P, 2, GH, DH])).then_inc(s_inv, 1)

            def normalise(k):
                g, qb = divmod(k, QB)
                dve.wait_ge(s_invt, k + 1)
                if k >= 1:
                    dve.wait_ge(s_olo, k)
                nc.vector.tensor_tensor(o32[:, :], o_ps[:, 0:2 * P], inv_sum_t[:, :], ALU.mult).then_inc(s_o32, 1)
                dve.wait_ge(s_o32, k + 1)
                nc.vector.tensor_copy(o16[:, 0, g, 2 * P * qb:2 * P * qb + 2 * P], o32[:, :]).then_inc(s_ohi, 1)

            def statistics(n):
                if n < 4:
                    dve.wait_ge(s_x[n % 2], 16 * (n // 2 + 1))
                source = x_in[:, n % 2, :, :] if n < 4 else x1[:, :, :]
                for t in range(2):
                    i = 2 * n + t
                    nc.vector.bn_stats(stats[:, i, :], source[:, t, :]).then_inc(s_stats, 1)
                for t in range(2):
                    i = 2 * n + t
                    dve.wait_ge(s_stats, i + 1)
                    nc.vector.bn_aggr(mean_var[:, i, :], stats[:, i, :]).then_inc(s_moments, 1)

            def negative_mean(n):
                dve.wait_ge(s_rstd, n + 1)
                nc.vector.scalar_tensor_tensor(
                    out=neg_mean[:, 2 * n:2 * n + 2], in0=mean_var[:, 2 * n:2 * n + 2, 0], scalar=-1.0,
                    in1=rstd[:, 2 * n:2 * n + 2], op0=ALU.mult, op1=ALU.mult).then_inc(s_negmean, 1)

            def h_hi(n):
                dve.wait_ge(s_relu, n + 1)
                if n >= 1:
                    dve.wait_ge(s_side, (4 * n - 3) if n < 5 else 4 * n - 2)
                nc.vector.tensor_copy(h16[:, 0, :, :], h32[:, :, :]).then_inc(s_hhi, 1)

            def qk_hi(n, which):
                dve.wait_ge(s_qk32, 2 * n + which + 1)
                nc.vector.tensor_copy(qk_next[:, which, 0, :, 2 * P * n:2 * P * n + 2 * P],
                                      qk32[:, which, :, :]).then_inc(s_qkhi, 1)

            def evict_v(n):
                dve.wait_ge(s_side, 4 * n + 4)
                nc.vector.scalar_tensor_tensor(
                    out=v_next[:, 2 * n:2 * n + 2, :], in0=side_ps[:, :].rearrange("p (t c) -> p t c", t=2),
                    scalar=1.0 / W_SCALE, in1=bias_v[:, None, :].to_broadcast([P, 2, D]), op0=ALU.mult,
                    op1=ALU.add).then_inc(s_v, 1)

            def first_residual(j):
                dve.wait_ge(s_side, 16 + 4 * j + 1)
                dve.wait_ge(s_xbias, j + 1)
                if j >= 1:
                    dve.wait_ge(s_relu, 4 + j)
                    dve.wait_ge(s_base, 2 * j)
                nc.vector.scalar_tensor_tensor(
                    out=x1[:, :, :], in0=side_ps[:, :].rearrange("p (t c) -> p t c", t=2), scalar=1.0 / W_SCALE,
                    in1=x_in[:, j % 2, :, :], op0=ALU.mult, op1=ALU.add).then_inc(s_x1done, 1)
                dve.wait_ge(s_x1done, j + 1)

            def message_rest(j, t):
                i = 2 * j + t
                dve.wait_ge(s_msghi, i + 1)
                if i >= 1:
                    dve.wait_ge(s_base, i)
                nc.vector.scalar_tensor_tensor(out=self32[:, :], in0=side_ps[:, 0:D], scalar=1.0 / W_SCALE,
                                               in1=bias_msg[:, :], op0=ALU.mult, op1=ALU.add).then_inc(s_self, 1)
                nc.vector.scalar_tensor_tensor(out=msg16[:, i, 1, :], in0=side_ps[:, D:2 * D], scalar=1.0,
                                               in1=msg16[:, i, 0, :], op0=ALU.mult,
                                               op1=ALU.subtract).then_inc(s_msglo, 1)
                dve.wait_ge(s_self, i + 1)
                nc.vector.scalar_tensor_tensor(out=base[:, i, :], in0=self32[:, :], scalar=deg[:, i:i + 1],
                                               in1=x1[:, t, :], op0=ALU.mult, op1=ALU.add).then_inc(s_base, 1)

            def result(i):
                dve.wait_ge(s_sums, i + 1)
                if i == 0:
                    dve.wait_ge(s_base, NT)
                if i >= 2:
                    dve.wait_ge(s_stored[i % 2], 16 * (i // 2))
                bank = s_ps[:, i // 2, 512 * (i % 2):512 * (i % 2) + 512].rearrange("p (t c) -> p t c", t=2)
                nc.vector.scalar_tensor_tensor(out=out32[:, i % 2, :, :], in0=bank, scalar=1.0 / W_SCALE,
                                               in1=base[:, 2 * i:2 * i + 2, :], op0=ALU.mult,
                                               op1=ALU.add).then_inc(s_out, 1)

            def front(s):
                if (n := front_pair(s, 0)) is not None:
                    statistics(n)
                if (n := front_pair(s, 1)) is not None:
                    negative_mean(n)
                if (n := front_pair(s, 2)) is not None:
                    h_hi(n)
                if (n := front_pair(s, 5)) is not None:
                    qk_hi(n, 0)
                if (n := front_pair(s, 6)) is not None:
                    qk_hi(n, 1)
                if (n := front_pair(s, 7)) is not None:
                    evict_v(n)

            dve.wait_ge(s_const, 16 * 5)
            nc.vector.tensor_copy(ident16[:, :], ident32[:, :]).then_inc(s_id16, 1)
            nc.vector.tensor_scalar(bias_qk[:, 0, :], bias_qk[:, 0, :], SCALE, None, ALU.mult).then_inc(s_id16, 1)
            dve.wait_ge(s_whi, 1)
            nc.vector.scalar_tensor_tensor(out=w16[:, 1, :, :], in0=w_raw, scalar=W_SCALE, in1=w16[:, 0, :, :],
                                           op0=ALU.mult, op1=ALU.subtract).then_inc(s_wlo, 1)
            for s in range(32):
                front(s)
            for t in range(NT):
                dve.wait_ge(s_adjload[t], 16)
                nc.vector.tensor_scalar(mask_add[:, t, :], adj_raw[:, t, :], 0.0, NEG, ALU.is_equal,
                                        ALU.mult).then_inc(s_mask, 1)
                dve.wait_ge(s_adjtp, t + 1)
                nc.vector.tensor_copy(adj_t[:, :, P * t:P * t + P],
                                      t_ps[:, t % 2, :].bitcast(F16).rearrange("p (j q) -> p j q", j=NT)
                                      ).then_inc(s_adjt, 1)
            leave_round(dve, "dve")

            with dve.Fori(0, B):
                for s in range(STEPS):
                    if s < UNITS:
                        mask_scores(s)
                    if (k := block_at(s, -1)) is not None:
                        inverse_sums(k)
                    if 0 <= s - 2 < UNITS:
                        copy_half(s - 2)
                    if s == 4:
                        dve.wait_ge(s_op1, 16 * OP_DMAS)
                    front(s)
                    if (k := block_at(s, 1)) is not None:
                        normalise(k)
                    if (j := tail_pair(s, 3)) is not None:
                        first_residual(j)
                        statistics(4 + j)
                    if (j := tail_pair(s, 4)) is not None:
                        negative_mean(4 + j)
                    if (j := tail_pair(s, 5)) is not None:
                        h_hi(4 + j)
                    if (j := tail_pair(s, 7)) is not None:
                        message_rest(j, 0)
                    if (j := tail_pair(s, 8)) is not None:
                        message_rest(j, 1)
                for i in range(NT // 2):
                    result(i)
                leave_round(dve, "dve")

        @block.gpsimd
        def _(pool):
            def inverse_deviation(n):
                at = slice(2 * n, 2 * n + 2)
                pool.wait_ge(s_moments, 2 * n + 2)
                nc.gpsimd.tensor_scalar(var_eps[:, at], mean_var[:, at, 1], 1.0, EPS, ALU.mult,
                                        ALU.add).then_inc(s_vareps, 1)
                pool.wait_ge(s_vareps, n + 1)
                nc.gpsimd.tensor_tensor(rstd[:, at], var_eps[:, at], minus_half[:, :], ALU.pow).then_inc(s_rstd, 1)

            def h_lo(n):
                pool.wait_ge(s_hhi, n + 1)
                nc.gpsimd.tensor_tensor(h16[:, 1, :, :], h32[:, :, :], h16[:, 0, :, :],
                                        ALU.subtract).then_inc(s_hlo, 1)

            def qk_lo(n, which):
                at = slice(2 * P * n, 2 * P * n + 2 * P)
                pool.wait_ge(s_qkhi, 2 * n + which + 1)
                nc.gpsimd.tensor_tensor(qk_next[:, which, 1, :, at], qk32[:, which, :, :],
                                        qk_next[:, which, 0, :, at], ALU.subtract).then_inc(s_qklo, 1)

            def o_lo(k):
                g, qb = divmod(k, QB)
                at = slice(2 * P * qb, 2 * P * qb + 2 * P)
                pool.wait_ge(s_ohi, k + 1)
                nc.gpsimd.tensor_tensor(o16[:, 1, g, at], o32[:, :], o16[:, 0, g, at],
                                        ALU.subtract).then_inc(s_olo, 1)

            def x_bias(j):
                n = 4 + j
                pool.wait_ge(s_x[n % 2], 16 * (n // 2 + 1))
                for t in range(2):
                    op = nc.gpsimd.tensor_tensor(x_in[:, n % 2, t, :], x_in[:, n % 2, t, :], bias_o[:, :], ALU.add)
                op.then_inc(s_xbias, 1)

            def front(s):
                if (n := front_pair(s, 0)) is not None:
                    inverse_deviation(n)
                if (n := front_pair(s, 2)) is not None:
                    h_lo(n)
                if (n := front_pair(s, 5)) is not None:
                    qk_lo(n, 0)
                if (n := front_pair(s, 6)) is not None:
                    qk_lo(n, 1)

            def end_round(totals):
                pool.wait_ge(s_arrive, 4)
                for name, value in totals.items():
                    pool.wait_ge(data_sems[name], value)
                for name in totals:
                    pool.sem_clear(data_sems[name])
                pool.sem_clear(s_arrive)
                for s in go.values():
                    pool.sem_inc(s, 1)

            nc.gpsimd.memset(minus_half[:, :], -0.5).then_inc(s_half, 1)
            pool.wait_ge(s_half, 1)
            for s in range(32):
                front(s)
            end_round(SETUP_TOTALS)

            with pool.Fori(0, B):
                for s in range(STEPS):
                    front(s)
                    if (k := block_at(s, 1)) is not None:
                        o_lo(k)
                    if (j := tail_pair(s, 2)) is not None:
                        x_bias(j)
                    if (j := tail_pair(s, 3)) is not None:
                        inverse_deviation(4 + j)
                    if (j := tail_pair(s, 5)) is not None:
                        h_lo(4 + j)
                end_round(ROUND_TOTALS)


def kernel(x, adj, L0_gnn_Wq, L0_gnn_bq, L0_gnn_Wk, L0_gnn_bk, L0_gnn_Wv, L0_gnn_bv, L0_gnn_Wo, L0_gnn_bo,
           L1_gnn_W, L1_gnn_b):
    import numpy as np
    import concourse.bacc as bacc
    from concourse.bass_utils import run_bass_kernel_spmd

    W = np.asarray(L1_gnn_W)
    w_t = np.concatenate([np.asarray(w).T for w in (L0_gnn_Wq, L0_gnn_Wk, L0_gnn_Wv, L0_gnn_Wo, W[:, :D], W[:, D:])],
                         axis=1)
    b_qk = np.stack([np.asarray(L0_gnn_bq).reshape(KC, P), np.asarray(L0_gnn_bk).reshape(KC, P)]).transpose(2, 0, 1)
    arrays = {
        "in_x": x, "in_adj": adj, "in_w_t": w_t, "in_b_qk": b_qk,
        "in_b_v": np.asarray(L0_gnn_bv)[None], "in_b_o": np.asarray(L0_gnn_bo)[None],
        "in_b_msg": np.asarray(L1_gnn_b)[None], "in_ident": np.eye(P, dtype=np.float32),
    }
    arrays = {n: np.ascontiguousarray(a) for n, a in arrays.items()}
    nc = bacc.Bacc("TRN2", target_bir_lowering=False, num_devices=1)
    args = [nc.dram_tensor(n, a.shape, mybir.dt.from_np(a.dtype), kind="ExternalInput").ap()
            for n, a in arrays.items()]
    result = nc.dram_tensor("out", (B, N, D), F32, kind="ExternalOutput").ap()
    gnn_kernel(nc, *args, result)
    r = run_bass_kernel_spmd(nc, [arrays], core_ids=[0])
    return r.results[0]["out"]
```

```python
from contextlib import ExitStack

import concourse.bass as bass
from concourse import mybir

F32 = mybir.dt.float32
F16 = mybir.dt.float16
F8 = mybir.dt.float8e4
BF16 = mybir.dt.bfloat16
I32 = mybir.dt.int32
ALU = mybir.AluOpType
ACT = mybir.ActivationFunctionType
AX_X = mybir.AxisListType.X

B, N, D = 8, 1024, 256
HEADS, DH = 8, 32
P = 128
NT = N // P
KC = D // P
GH = P // DH
QB = 4
UNITS = HEADS * NT
BLOCKS = UNITS // 8
W_SCALE = 64.0
SCALE = float(DH) ** -0.5
EPS = 1e-5
NEG = -1e30
WQ, WK, WV, WO, WI = 0, D, 2 * D, 3 * D, 4 * D
W_COLS = 6 * D
TERMS = [(0, 0), (0, 1), (1, 0)]


def unit(u):
    return u // 32, (u // 8) % QB, (u // 2) % GH, u % 2


def gnn_kernel(nc, x, adj, w_t, b_qk, b_v, b_o, b_msg, ident, qk_dram, v_dram, out):
    with ExitStack() as ctx:
        def sb(name, shape, dt):
            return ctx.enter_context(nc.sbuf_tensor(name, shape, dt))

        def pb(name, shape, dt):
            return ctx.enter_context(nc.psum_tensor(name, shape, dt))

        ident32 = sb("ident32", [P, P], F32)
        ident16 = sb("ident16", [P, P], F16)
        w16 = sb("w16", [P, 2, KC, W_COLS], F16)
        bias_qk = sb("bias_qk", [P, 2, KC], F32)
        bias_v = sb("bias_v", [P, D], F32)
        bias_o = sb("bias_o", [P, D], F32)
        bias_msg = sb("bias_msg", [P, D], F32)
        minus_half = sb("minus_half", [P, 2], F32)
        mask_add = sb("mask_add", [P, NT, N], BF16)
        adj_t = sb("adj_t", [P, NT, N], F8)
        deg = sb("deg", [P, NT], F32)
        q_op = sb("q_op", [P, HEADS, N], F16)
        k_op = sb("k_op", [P, HEADS, N], F16)
        v_op = sb("v_op", [P, KC, NT, P], F32)
        qk16 = sb("qk16", [P, 2, 2, KC, 2 * P], F16)
        v32 = sb("v32", [P, 2, D], F32)
        probs = sb("probs", [P, 3, N], F32)
        probs_t = sb("probs_t", [P, 2, GH, NT, 2 * P], F32)
        neg_max = sb("neg_max", [P, UNITS], F32)
        row_sum = sb("row_sum", [P, UNITS], F32)
        inv_unit = sb("inv_unit", [P, 8], F32)
        inv_sum = sb("inv_sum", [P, 2, GH, DH], F32)
        inv_sum_t = sb("inv_sum_t", [P, 2 * P], F32)
        o32 = sb("o32", [P, 2 * P], F32)
        o16 = sb("o16", [P, 2, KC, N], F16)
        x_in = sb("x_in", [P, 2, 2, D], F32)
        x1 = sb("x1", [P, 2, D], F32)
        stats = sb("stats", [P, 16, 6], F32)
        mean_var = sb("mean_var", [P, 16, 2], F32)
        var_eps = sb("var_eps", [P, 16], F32)
        rstd = sb("rstd", [P, 16], F32)
        neg_mean = sb("neg_mean", [P, 16], F32)
        h32 = sb("h32", [P, 2, D], F32)
        h16 = sb("h16", [P, 2, 2, D], F16)
        h_t = sb("h_t", [P, 2, KC, 2 * P], F16)
        qk32 = sb("qk32", [P, KC, 2 * P], F32)
        msg16 = sb("msg16", [P, NT, 2, D], F16)
        self32 = sb("self32", [P, D], F32)
        base = sb("base", [P, NT, D], F32)

        adj_raw = probs_t[:, 0, :, :, :].bitcast(I32).rearrange("p h k q -> p (h k q)")\
                                        .rearrange("p (t n) -> p t n", t=NT)
        adj16 = probs_t[:, 1, 0, 0:4, :].bitcast(F16).rearrange("p k q -> p (k q)").rearrange("p (t n) -> p t n", t=2)
        w_raw = probs[:, :, :].rearrange("p a n -> p (a n)").rearrange("p (c n) -> p c n", c=KC)

        s_ps = pb("s_ps", [P, 2, N], F32)
        t_ps = pb("t_ps", [P, 2, 512], F32)
        o_ps = pb("o_ps", [P, 512], F32)
        side_ps = pb("side_ps", [P, 512], F32)

        sems = {}

        def sem(name):
            sems[name] = ctx.enter_context(nc.semaphore(name))
            return sems[name]

        s_const = sem("s_const")
        s_wload = sem("s_wload")
        s_adjload = [sem(f"s_adjload{t}") for t in range(NT)]
        s_id16 = sem("s_id16")
        s_half = sem("s_half")
        s_whi = sem("s_whi")
        s_wlo = sem("s_wlo")
        s_adj16 = sem("s_adj16")
        s_mask = sem("s_mask")
        s_adjtp = sem("s_adjtp")
        s_adjt = sem("s_adjt")
        s_scores = sem("s_scores")
        s_masked = sem("s_masked")
        s_exp = sem("s_exp")
        s_tp = sem("s_tp")
        s_copy0 = sem("s_copy0")
        s_copy1 = sem("s_copy1")
        s_pv = sem("s_pv")
        s_invunit = sem("s_invunit")
        s_inv = sem("s_inv")
        s_invtp = sem("s_invtp")
        s_invt = sem("s_invt")
        s_o32 = sem("s_o32")
        s_ohi = sem("s_ohi")
        s_olo = sem("s_olo")
        s_x = [sem("s_x0"), sem("s_x1")]
        s_stats = sem("s_stats")
        s_moments = sem("s_moments")
        s_vareps = sem("s_vareps")
        s_rstd = sem("s_rstd")
        s_negmean = sem("s_negmean")
        s_relu = sem("s_relu")
        s_hhi = sem("s_hhi")
        s_hlo = sem("s_hlo")
        s_side = sem("s_side")
        s_ht = sem("s_ht")
        s_qk32 = sem("s_qk32")
        s_qkhi = sem("s_qkhi")
        s_qklo = sem("s_qklo")
        s_v = sem("s_v")
        s_qkkept = [sem("s_qkept"), sem("s_kkept")]
        s_vkept = sem("s_vkept")
        s_xbias = sem("s_xbias")
        s_x1done = sem("s_x1done")
        s_msghi = sem("s_msghi")
        s_msglo = sem("s_msglo")
        s_self = sem("s_self")
        s_base = sem("s_base")
        s_sums = sem("s_sums")
        s_out = sem("s_out")
        s_stored = sem("s_stored")
        s_op0 = sem("s_op0")
        s_op1 = sem("s_op1")
        data_sems = dict(sems)
        s_arrive = sem("s_arrive")
        go = {e: sem(f"s_go_{e}") for e in ("pe", "act", "dve", "sp")}

        OP_DMAS = 2 * 4 + 1
        x_t = x.rearrange("b (t p) c -> b p t c", p=P)
        out_t = out.rearrange("b (t p) c -> b p t c", p=P)
        qk_rows = [qk_dram[which].rearrange("a g p n -> p (a g) n") for which in range(2)]
        v_rows = v_dram.rearrange("(t p) c -> p t c", p=P)


        FRONT_TOTALS = {
            "s_x0": 32, "s_x1": 32, "s_stats": 8, "s_moments": 8, "s_vareps": 4, "s_rstd": 4, "s_negmean": 4,
            "s_relu": 4, "s_hhi": 4, "s_hlo": 4, "s_side": 16, "s_ht": 4, "s_qk32": 8,
            "s_qkhi": 8, "s_qklo": 8, "s_v": 4, "s_qkept": 64, "s_kkept": 64, "s_vkept": 64,
            "s_op0": 16 * OP_DMAS,
        }
        SETUP_TOTALS = FRONT_TOTALS | {
            "s_const": 16 * 5, "s_wload": 16, "s_id16": 2, "s_half": 1, "s_whi": 1, "s_wlo": 1, "s_adj16": NT,
            "s_mask": NT, "s_adjtp": NT, "s_adjt": NT,
        } | {f"s_adjload{t}": 16 for t in range(NT)}
        ROUND_TOTALS = FRONT_TOTALS | {
            "s_scores": UNITS, "s_masked": UNITS, "s_exp": UNITS, "s_tp": 2 * UNITS, "s_copy0": UNITS,
            "s_copy1": UNITS, "s_pv": BLOCKS, "s_invunit": BLOCKS, "s_inv": BLOCKS, "s_invtp": BLOCKS, "s_invt": BLOCKS,
            "s_o32": BLOCKS, "s_ohi": BLOCKS, "s_olo": BLOCKS,
            "s_x0": 64, "s_x1": 64, "s_stats": 16, "s_moments": 16, "s_vareps": 8, "s_rstd": 8, "s_negmean": 8,
            "s_relu": 8, "s_hhi": 8, "s_hlo": 8, "s_side": 32, "s_ht": 8,
            "s_xbias": 4, "s_x1done": 4, "s_msghi": 8, "s_msglo": 8, "s_self": 8, "s_base": 8,
            "s_sums": 4, "s_out": 4, "s_stored": 64, "s_op1": 16 * OP_DMAS,
        }

        PV_TILES = [(0, 1), (2, 3), (4,), (5,), (6,), (7,)]
        PV_FIRST, PV_LAST = 10, 15
        STEPS = UNITS + 16

        def pv_tiles(s):
            k, i = divmod(s - PV_FIRST, 8)
            return (k, PV_TILES[i]) if 0 <= k < BLOCKS and i < len(PV_TILES) else None

        def front_pair(s, offset):
            n, o = divmod(s - offset, 8)
            return n if o == 0 and 0 <= n < 4 else None

        def tail_pair(s, offset):
            j, o = divmod(s - offset - 8 * QB - PV_LAST, 8)
            return j if o == 0 and 0 <= j < 4 else None

        def block_at(s, offset):
            k, o = divmod(s - offset - PV_LAST, 8)
            return k if o == 0 and 0 <= k < BLOCKS else None

        def leave_round(eng, name):
            eng.sem_inc(s_arrive, 1)
            eng.wait_ge(go[name], 1)
            eng.sem_clear(go[name])

        block = ctx.enter_context(nc.Block())

        @block.sync
        def _(sp):
            def load_front(n, b_next):
                if n >= 2:
                    sp.wait_ge(s_relu, n - 1)
                sp.dma_start(x_in[:, n % 2, :, :], x_pair(b_next, n)).then_inc(s_x[n % 2], 16)

            def x_pair(b, n):
                return x_t[bass.ds(b, 1), :, 2 * n:2 * n + 2, :].rearrange("b p t c -> p (b t) c")

            def load_tail(j, b):
                n = QB + j
                if j < 2:
                    sp.wait_ge(s_relu, n - 1)
                else:
                    sp.wait_ge(s_x1done, j - 1)
                sp.dma_start(x_in[:, n % 2, :, :], x_pair(b, j)).then_inc(s_x[n % 2], 16)

            def keep_pair(n):
                for which in range(2):
                    sp.wait_ge(s_qklo, 2 * n + which + 1)
                    sp.dma_start(qk_rows[which][:, :, 2 * P * n:2 * P * n + 2 * P],
                                 qk16[:, which, :, :, :].rearrange("p a g n -> p (a g) n")
                                 ).then_inc(s_qkkept[which], 16)
                sp.wait_ge(s_v, n + 1)
                sp.dma_start(v_rows[:, 2 * n:2 * n + 2, :], v32[:, :, :]).then_inc(s_vkept, 16)

            def load_operands(g, done):
                for r, (q_part, k_part) in enumerate([(0, 0), (0, 1), (1, 0), (1, 1)]):
                    for which, part, to in ((0, q_part, q_op), (1, k_part, k_op)):
                        sp.dma_start(to[DH * r:DH * r + DH, GH * g:GH * g + GH, :],
                                     qk_dram[which, part, g].rearrange("(h p) n -> p h n", p=DH)).then_inc(done, 16)
                sp.dma_start(v_op[:, g, :, :], v_rows[:, :, P * g:P * g + P]).then_inc(done, 16)

            def next_kept():
                for kept in (*s_qkkept, s_vkept):
                    sp.wait_ge(kept, 64)

            sp.dma_start(w_raw, w_t.rearrange("(c p) n -> p c n", p=P)).then_inc(s_wload, 16)
            sp.dma_start(ident32[:, :], ident).then_inc(s_const, 16)
            sp.dma_start(bias_qk[:, :, :], b_qk).then_inc(s_const, 16)
            for to, of in ((bias_v, b_v), (bias_o, b_o), (bias_msg, b_msg)):
                sp.dma_start(to[:, :], of.to_broadcast([P, D])).then_inc(s_const, 16)
            load_front(0, 0)
            load_front(1, 0)
            for t in range(NT):
                sp.dma_start(adj_raw[:, t, :], adj[P * t:P * t + P, :]).then_inc(s_adjload[t], 16)
            keep_pair(0)
            load_front(2, 0)
            keep_pair(1)
            load_front(3, 0)
            keep_pair(2)
            keep_pair(3)
            next_kept()
            load_operands(0, s_op0)
            leave_round(sp, "sp")

            with sp.Fori(0, B) as b:
                b_next = (b + 1) % B
                load_front(0, b_next)
                load_front(1, b_next)
                load_operands(1, s_op1)
                sp.wait_ge(s_op1, 16 * OP_DMAS)
                keep_pair(0)
                load_front(2, b_next)
                keep_pair(1)
                load_front(3, b_next)
                keep_pair(2)
                load_tail(0, b)
                keep_pair(3)
                load_tail(1, b)
                next_kept()
                sp.wait_ge(s_scores, UNITS // 2)
                sp.wait_ge(s_pv, QB)
                load_operands(0, s_op0)
                load_tail(2, b)
                load_tail(3, b)
                for i in range(NT // 2):
                    sp.wait_ge(s_out, i + 1)
                    sp.dma_start(out_t[bass.ds(b, 1), :, 2 * i:2 * i + 2, :].rearrange("b p t c -> p (b t) c"),
                                 base[:, 2 * i:2 * i + 2, :]).then_inc(s_stored, 16)
                leave_round(sp, "sp")

        @block.tensor
        def _(pe):
            def adj_transposes(t):
                pe.wait_ge(s_adj16, t + 1)
                if t >= 2:
                    pe.wait_ge(s_adjt, t - 1)
                bank = t_ps[:, t % 2, :].bitcast(F16)
                for j in range(NT):
                    mm = pe.transpose(bank[:, P * j:P * j + P], adj16[:, t % 2, P * j:P * j + P], ident16[:, :])
                mm.then_inc(s_adjtp, 1)

            def scores(u):
                g, qb, hh, qt = unit(u)
                if u >= 2:
                    pe.wait_ge(s_masked, u - 1)
                if u == UNITS // 2:
                    pe.wait_ge(s_op1, 16 * OP_DMAS)
                h = GH * g + hh
                at = (2 * qb + qt) * P
                for c in range(2):
                    mm = pe.matmul(s_ps[:, u % 2, 512 * c:512 * c + 512], q_op[:, h, at:at + P],
                                   k_op[:, h, 512 * c:512 * c + 512], start=True, stop=True)
                mm.then_inc(s_scores, 1)

            def transposes(u):
                pe.wait_ge(s_exp, u + 1)
                for half in range(2):
                    if u >= 1:
                        pe.wait_ge((s_copy0, s_copy1)[half], u)
                    for j in range(4):
                        k = 4 * half + j
                        mm = pe.transpose(t_ps[:, half, P * j:P * j + P], probs[:, u % 3, P * k:P * k + P],
                                          ident32[:, :])
                    mm.then_inc(s_tp, 1)

            def times_v(k, tiles):
                g = k // QB
                if tiles[0] == 0:
                    pe.wait_ge(s_copy0, 8 * k + 8)
                    pe.wait_ge(s_copy1, 8 * k + 8)
                    if k >= 1:
                        pe.wait_ge(s_o32, k)
                for t in tiles:
                    for hh in range(GH):
                        at = slice(DH * hh, DH * hh + DH)
                        mm = pe.matmul(o_ps[at, 0:2 * P], v_op[:, g, t, at], probs_t[:, k % 2, hh, t, :],
                                       start=(t == 0), stop=(t == NT - 1))
                if tiles[-1] == NT - 1:
                    mm.then_inc(s_pv, 1)

            def turn_inverse(k):
                pe.wait_ge(s_inv, k + 1)
                for qt in range(2):
                    mm = pe.transpose(o_ps[:, 2 * P + P * qt:2 * P + P * qt + P],
                                      inv_sum[:, qt, :, :].rearrange("p h d -> p (h d)"), ident32[:, :])
                mm.then_inc(s_invtp, 1)

            def turn_h(n):
                pe.wait_ge(s_hhi, n + 1)
                pe.wait_ge(s_hlo, n + 1)
                if n >= 4:
                    pe.wait_ge(s_x1done, n - 3)
                elif n >= 1:
                    pe.wait_ge(s_v, n)
                bank = side_ps[:, :].bitcast(F16).rearrange("p (a c n) -> p a c n", a=2, c=KC)
                for part in range(2):
                    for c in range(KC):
                        for t in range(2):
                            mm = pe.transpose(bank[:, part, c, P * t:P * t + P], h16[:, part, t, P * c:P * c + P],
                                              ident16[:, :])
                mm.then_inc(s_side, 1)

            def q_or_k(n, which):
                if which == 0:
                    pe.wait_ge(s_ht, n + 1)
                else:
                    pe.wait_ge(s_qk32, 2 * n + 1)
                for g in range(KC):
                    col = (WQ, WK)[which] + P * g
                    for i, (w_part, h_part) in enumerate(TERMS):
                        for c in range(KC):
                            mm = pe.matmul(side_ps[:, 2 * P * g:2 * P * g + 2 * P], w16[:, w_part, c, col:col + P],
                                           h_t[:, h_part, c, :], start=(i + c == 0), stop=(i == 2 and c == KC - 1))
                mm.then_inc(s_side, 1)

            def v_pair(n):
                pe.wait_ge(s_qk32, 2 * n + 2)
                for t in range(2):
                    for i, (h_part, w_part) in enumerate(TERMS):
                        for c in range(KC):
                            mm = pe.matmul(side_ps[:, D * t:D * t + D], h_t[:, h_part, c, P * t:P * t + P],
                                           w16[:, w_part, c, WV:WV + D], start=(i + c == 0),
                                           stop=(i == 2 and c == KC - 1))
                mm.then_inc(s_side, 1)

            def messages_read(tiles):
                pe.wait_ge(s_msghi, tiles)
                pe.wait_ge(s_msglo, tiles)

            def output_product(j):
                pe.wait_ge(s_ohi, QB + j + 1)
                pe.wait_ge(s_olo, QB + j + 1)
                if j == 0:
                    pe.wait_ge(s_v, 4)
                else:
                    messages_read(2 * j)
                for t in range(2):
                    at = (2 * j + t) * P
                    for i, (o_part, w_part) in enumerate(TERMS):
                        for c in range(KC):
                            mm = pe.matmul(side_ps[:, D * t:D * t + D], o16[:, o_part, c, at:at + P],
                                           w16[:, w_part, c, WO:WO + D], start=(i + c == 0),
                                           stop=(i == 2 and c == KC - 1))
                mm.then_inc(s_side, 1)

            def messages(j, t):
                if t == 0:
                    pe.wait_ge(s_ht, 4 + j + 1)
                else:
                    messages_read(2 * j + 1)
                for i, (h_part, w_part) in enumerate(TERMS):
                    for c in range(KC):
                        mm = pe.matmul(side_ps[:, :], h_t[:, h_part, c, P * t:P * t + P],
                                       w16[:, w_part, c, WI:WI + 2 * D], start=(i + c == 0),
                                       stop=(i == 2 and c == KC - 1))
                mm.then_inc(s_side, 1)

            def neighbour_sums(j_tiles):
                pe.wait_ge(s_msghi, j_tiles[-1] + 1)
                pe.wait_ge(s_msglo, j_tiles[-1] + 1)
                if j_tiles[0] == 0:
                    pe.wait_ge(s_masked, UNITS)
                for i in range(NT):
                    for j in j_tiles:
                        for part in range(2):
                            mm = pe.matmul(s_ps[:, i // 4, D * (i % 4):D * (i % 4) + D], adj_t[:, j, P * i:P * i + P],
                                           msg16[:, j, part, :], start=(j == 0 and part == 0 and i % 2 == 0),
                                           stop=(j == NT - 1 and part == 1), skip_group_check=True)
                    if j_tiles[-1] == NT - 1 and i % 2 == 1:
                        mm.then_inc(s_sums, 1)

            def front(s):
                if (n := front_pair(s, 5)) is not None:
                    turn_h(n)
                if (n := front_pair(s, 6)) is not None:
                    q_or_k(n, 0)
                if (n := front_pair(s, 7)) is not None:
                    q_or_k(n, 1)
                if (n := front_pair(s, 8)) is not None:
                    v_pair(n)

            pe.wait_ge(s_id16, 2)
            pe.wait_ge(s_whi, 1)
            pe.wait_ge(s_wlo, 1)
            for s in range(40):
                front(s)
            for t in range(NT):
                adj_transposes(t)
            leave_round(pe, "pe")

            with pe.Fori(0, B):
                for s in range(STEPS):
                    if s < UNITS:
                        scores(s)
                    if 0 <= s - 2 < UNITS:
                        transposes(s - 2)
                    if (piece := pv_tiles(s)) is not None:
                        times_v(*piece)
                    if (k := block_at(s, 0)) is not None:
                        turn_inverse(k)
                    front(s)
                    if (j := tail_pair(s, 3)) is not None:
                        output_product(j)
                    if (j := tail_pair(s, 6)) is not None:
                        turn_h(4 + j)
                    if (j := tail_pair(s, 7)) is not None:
                        messages(j, 0)
                    if (j := tail_pair(s, 8)) is not None:
                        messages(j, 1)
                    if s == UNITS + 8:
                        neighbour_sums(range(0, 2))
                    if s == UNITS + 11:
                        neighbour_sums(range(2, 6))
                neighbour_sums(range(6, 8))
                leave_round(pe, "pe")

        @block.scalar
        def _(act):
            def exponentials(u):
                act.wait_ge(s_masked, u + 1)
                nc.scalar.activation(probs[:, u % 3, :], probs[:, u % 3, :], ACT.Exp, bias=neg_max[:, u:u + 1],
                                     scale=-1.0, accum_out=row_sum[:, u:u + 1]).then_inc(s_exp, 1)

            def copy_half(u):
                _, _, hh, qt = unit(u)
                act.wait_ge(s_tp, 2 * u + 1)
                nc.scalar.copy(probs_t[:, u // 8 % 2, hh, 0:4, P * qt:P * qt + P],
                               t_ps[:, 0, :].rearrange("p (k q) -> p k q", k=4)).then_inc(s_copy0, 1)

            def copy_inverse(k):
                act.wait_ge(s_invtp, k + 1)
                if k >= 1:
                    act.wait_ge(s_o32, k)
                nc.scalar.copy(inv_sum_t[:, :], o_ps[:, 2 * P:4 * P]).then_inc(s_invt, 1)

            def relu(n):
                act.wait_ge(s_negmean, n + 1)
                if n >= 1:
                    act.wait_ge(s_hhi, n)
                    act.wait_ge(s_hlo, n)
                source = x_in[:, n % 2, :, :] if n < 4 else x1[:, :, :]
                for t in range(2):
                    i = 2 * n + t
                    op = nc.scalar.activation(h32[:, t, :], source[:, t, :], ACT.Relu, bias=neg_mean[:, i:i + 1],
                                              scale=rstd[:, i:i + 1])
                op.then_inc(s_relu, 1)

            def copy_h_t(n):
                i = 4 * n if n < 4 else 4 * n + 1
                act.wait_ge(s_side, i + 1)
                nc.scalar.copy(h_t[:, :, :, :].rearrange("p a c n -> p (a c n)"),
                               side_ps[:, :].bitcast(F16)).then_inc(s_ht, 1)

            def evict_qk(n, which):
                act.wait_ge(s_side, 4 * n + 2 + which)
                if n + which >= 1:
                    act.wait_ge(s_qkhi, 2 * n + which)
                    act.wait_ge(s_qklo, 2 * n + which)
                for g in range(KC):
                    op = nc.scalar.activation(qk32[:, g, :], side_ps[:, 2 * P * g:2 * P * g + 2 * P],
                                              ACT.Identity, bias=bias_qk[:, which, g:g + 1],
                                              scale=(SCALE if which == 0 else 1.0) / W_SCALE)
                op.then_inc(s_qk32, 1)

            def message_hi(j, t):
                act.wait_ge(s_side, 16 + 4 * j + 3 + t)
                nc.scalar.copy(msg16[:, 2 * j + t, 0, :], side_ps[:, D:2 * D]).then_inc(s_msghi, 1)

            def front(s):
                if (n := front_pair(s, 3)) is not None:
                    relu(n)
                if (n := front_pair(s, 5)) is not None:
                    copy_h_t(n)
                if (n := front_pair(s, 6)) is not None:
                    evict_qk(n, 0)
                if (n := front_pair(s, 7)) is not None:
                    evict_qk(n, 1)

            act.wait_ge(s_wload, 16)
            nc.scalar.activation(w16[:, 0, :, :], w_raw, ACT.Copy, scale=W_SCALE).then_inc(s_whi, 1)
            act.wait_ge(s_id16, 2)
            for s in range(40):
                front(s)
            for t in range(NT):
                act.wait_ge(s_adjload[t], 16)
                if t >= 2:
                    act.wait_ge(s_adjtp, t - 1)
                nc.scalar.activation(adj16[:, t % 2, :], adj_raw[:, t, :], ACT.Copy,
                                     accum_out=deg[:, t:t + 1]).then_inc(s_adj16, 1)
            leave_round(act, "act")

            with act.Fori(0, B):
                for s in range(STEPS):
                    if 0 <= s - 2 < UNITS:
                        copy_half(s - 2)
                    if (k := block_at(s, 1)) is not None:
                        copy_inverse(k)
                    if s < UNITS:
                        exponentials(s)
                    front(s)
                    if (j := tail_pair(s, 4)) is not None:
                        relu(4 + j)
                    if (j := tail_pair(s, 6)) is not None:
                        copy_h_t(4 + j)
                    if (j := tail_pair(s, 7)) is not None:
                        message_hi(j, 0)
                    if (j := tail_pair(s, 8)) is not None:
                        message_hi(j, 1)
                leave_round(act, "act")

        @block.vector
        def _(dve):
            def mask_scores(u):
                _, qb, _, qt = unit(u)
                dve.wait_ge(s_scores, u + 1)
                if u >= 3:
                    dve.wait_ge(s_tp, 2 * (u - 3) + 2)
                nc.vector.tensor_tensor_reduce(
                    out=probs[:, u % 3, :], in0=s_ps[:, u % 2, :], in1=mask_add[:, 2 * qb + qt, :], scale=-1.0,
                    scalar=3e38, op0=ALU.add, op1=ALU.min, accum_out=neg_max[:, u:u + 1]).then_inc(s_masked, 1)

            def copy_half(u):
                _, _, hh, qt = unit(u)
                dve.wait_ge(s_tp, 2 * u + 2)
                nc.vector.tensor_copy(probs_t[:, u // 8 % 2, hh, 4:8, P * qt:P * qt + P],
                                      t_ps[:, 1, :].rearrange("p (k q) -> p k q", k=4)).then_inc(s_copy1, 1)

            def inverse_sums(k):
                dve.wait_ge(s_exp, 8 * k + 8)
                if k >= 1:
                    dve.wait_ge(s_inv, k)
                nc.vector.reciprocal(inv_unit[:, :], row_sum[:, 8 * k:8 * k + 8]).then_inc(s_invunit, 1)

            def normalise(k):
                g, qb = divmod(k, QB)
                dve.wait_ge(s_invt, k + 1)
                if k >= 1:
                    dve.wait_ge(s_olo, k)
                nc.vector.tensor_tensor(o32[:, :], o_ps[:, 0:2 * P], inv_sum_t[:, :], ALU.mult).then_inc(s_o32, 1)
                dve.wait_ge(s_o32, k + 1)
                nc.vector.tensor_copy(o16[:, 0, g, 2 * P * qb:2 * P * qb + 2 * P], o32[:, :]).then_inc(s_ohi, 1)

            def statistics(n):
                if n < 4:
                    dve.wait_ge(s_x[n % 2], 16 * (n // 2 + 1))
                source = x_in[:, n % 2, :, :] if n < 4 else x1[:, :, :]
                for t in range(2):
                    i = 2 * n + t
                    nc.vector.bn_stats(stats[:, i, :], source[:, t, :]).then_inc(s_stats, 1)
                for t in range(2):
                    i = 2 * n + t
                    dve.wait_ge(s_stats, i + 1)
                    nc.vector.bn_aggr(mean_var[:, i, :], stats[:, i, :]).then_inc(s_moments, 1)

            def negative_mean(n):
                dve.wait_ge(s_rstd, n + 1)
                nc.vector.scalar_tensor_tensor(
                    out=neg_mean[:, 2 * n:2 * n + 2], in0=mean_var[:, 2 * n:2 * n + 2, 0], scalar=-1.0,
                    in1=rstd[:, 2 * n:2 * n + 2], op0=ALU.mult, op1=ALU.mult).then_inc(s_negmean, 1)

            def h_hi(n):
                dve.wait_ge(s_relu, n + 1)
                if n >= 1:
                    dve.wait_ge(s_side, (4 * n - 3) if n < 5 else 4 * n - 2)
                nc.vector.tensor_copy(h16[:, 0, :, :], h32[:, :, :]).then_inc(s_hhi, 1)

            def qk_hi(n, which):
                dve.wait_ge(s_qk32, 2 * n + which + 1)
                if n >= 1:
                    dve.wait_ge(s_qkkept[which], 16 * n)
                nc.vector.tensor_copy(qk16[:, which, 0, :, :], qk32[:, :, :]).then_inc(s_qkhi, 1)

            def evict_v(n):
                dve.wait_ge(s_side, 4 * n + 4)
                if n >= 1:
                    dve.wait_ge(s_vkept, 16 * n)
                nc.vector.scalar_tensor_tensor(
                    out=v32[:, :, :], in0=side_ps[:, :].rearrange("p (t c) -> p t c", t=2),
                    scalar=1.0 / W_SCALE, in1=bias_v[:, None, :].to_broadcast([P, 2, D]), op0=ALU.mult,
                    op1=ALU.add).then_inc(s_v, 1)

            def first_residual(j):
                dve.wait_ge(s_side, 16 + 4 * j + 1)
                dve.wait_ge(s_xbias, j + 1)
                if j >= 1:
                    dve.wait_ge(s_relu, 4 + j)
                    dve.wait_ge(s_base, 2 * j)
                nc.vector.scalar_tensor_tensor(
                    out=x1[:, :, :], in0=side_ps[:, :].rearrange("p (t c) -> p t c", t=2), scalar=1.0 / W_SCALE,
                    in1=x_in[:, j % 2, :, :], op0=ALU.mult, op1=ALU.add).then_inc(s_x1done, 1)
                dve.wait_ge(s_x1done, j + 1)

            def message_rest(j, t):
                i = 2 * j + t
                dve.wait_ge(s_msghi, i + 1)
                if i >= 1:
                    dve.wait_ge(s_base, i)
                nc.vector.scalar_tensor_tensor(out=self32[:, :], in0=side_ps[:, 0:D], scalar=1.0 / W_SCALE,
                                               in1=bias_msg[:, :], op0=ALU.mult, op1=ALU.add).then_inc(s_self, 1)
                nc.vector.scalar_tensor_tensor(out=msg16[:, i, 1, :], in0=side_ps[:, D:2 * D], scalar=1.0,
                                               in1=msg16[:, i, 0, :], op0=ALU.mult,
                                               op1=ALU.subtract).then_inc(s_msglo, 1)
                dve.wait_ge(s_self, i + 1)
                nc.vector.scalar_tensor_tensor(out=base[:, i, :], in0=self32[:, :], scalar=deg[:, i:i + 1],
                                               in1=x1[:, t, :], op0=ALU.mult, op1=ALU.add).then_inc(s_base, 1)

            def result(i):
                dve.wait_ge(s_sums, i + 1)
                if i == 0:
                    dve.wait_ge(s_base, NT)
                bank = s_ps[:, i // 2, 512 * (i % 2):512 * (i % 2) + 512].rearrange("p (t c) -> p t c", t=2)
                nc.vector.scalar_tensor_tensor(out=base[:, 2 * i:2 * i + 2, :], in0=bank, scalar=1.0 / W_SCALE,
                                               in1=base[:, 2 * i:2 * i + 2, :], op0=ALU.mult,
                                               op1=ALU.add).then_inc(s_out, 1)

            def front(s):
                if (n := front_pair(s, 1)) is not None:
                    statistics(n)
                if (n := front_pair(s, 2)) is not None:
                    negative_mean(n)
                if (n := front_pair(s, 3)) is not None:
                    h_hi(n)
                if (n := front_pair(s, 6)) is not None:
                    qk_hi(n, 0)
                if (n := front_pair(s, 7)) is not None:
                    qk_hi(n, 1)
                if (n := front_pair(s, 8)) is not None:
                    evict_v(n)

            dve.wait_ge(s_const, 16 * 5)
            nc.vector.tensor_copy(ident16[:, :], ident32[:, :]).then_inc(s_id16, 1)
            nc.vector.tensor_scalar(bias_qk[:, 0, :], bias_qk[:, 0, :], SCALE, None, ALU.mult).then_inc(s_id16, 1)
            dve.wait_ge(s_whi, 1)
            nc.vector.scalar_tensor_tensor(out=w16[:, 1, :, :], in0=w_raw, scalar=W_SCALE, in1=w16[:, 0, :, :],
                                           op0=ALU.mult, op1=ALU.subtract).then_inc(s_wlo, 1)
            for s in range(40):
                front(s)
            for t in range(NT):
                dve.wait_ge(s_adjload[t], 16)
                nc.vector.tensor_scalar(mask_add[:, t, :], adj_raw[:, t, :], 0.0, NEG, ALU.is_equal,
                                        ALU.mult).then_inc(s_mask, 1)
                dve.wait_ge(s_adjtp, t + 1)
                nc.vector.tensor_copy(adj_t[:, :, P * t:P * t + P],
                                      t_ps[:, t % 2, :].bitcast(F16).rearrange("p (j q) -> p j q", j=NT), saturate=False
                                      ).then_inc(s_adjt, 1)
            leave_round(dve, "dve")

            with dve.Fori(0, B):
                for s in range(STEPS):
                    if s < UNITS:
                        mask_scores(s)
                    if (k := block_at(s, -5)) is not None:
                        inverse_sums(k)
                    if 0 <= s - 2 < UNITS:
                        copy_half(s - 2)
                    front(s)
                    if (k := block_at(s, 1)) is not None:
                        normalise(k)
                    if (j := tail_pair(s, 3)) is not None:
                        first_residual(j)
                        statistics(4 + j)
                    if (j := tail_pair(s, 4)) is not None:
                        negative_mean(4 + j)
                    if (j := tail_pair(s, 5)) is not None:
                        h_hi(4 + j)
                    if (j := tail_pair(s, 7)) is not None:
                        message_rest(j, 0)
                    if (j := tail_pair(s, 8)) is not None:
                        message_rest(j, 1)
                for i in range(NT // 2):
                    result(i)
                leave_round(dve, "dve")

        @block.gpsimd
        def _(pool):
            def inverse_deviation(n):
                at = slice(2 * n, 2 * n + 2)
                pool.wait_ge(s_moments, 2 * n + 2)
                nc.gpsimd.tensor_scalar(var_eps[:, at], mean_var[:, at, 1], 1.0, EPS, ALU.mult,
                                        ALU.add).then_inc(s_vareps, 1)
                pool.wait_ge(s_vareps, n + 1)
                nc.gpsimd.tensor_tensor(rstd[:, at], var_eps[:, at], minus_half[:, :], ALU.pow).then_inc(s_rstd, 1)

            def repeat_inverse(k):
                pool.wait_ge(s_invunit, k + 1)
                if k >= 1:
                    pool.wait_ge(s_invtp, k)
                units = inv_unit[:, :].rearrange("p (h q) -> p q h", q=2)
                nc.gpsimd.tensor_copy(inv_sum[:, :, :, :],
                                      units[:, :, :, None].to_broadcast([P, 2, GH, DH])).then_inc(s_inv, 1)

            def h_lo(n):
                pool.wait_ge(s_hhi, n + 1)
                nc.gpsimd.tensor_tensor(h16[:, 1, :, :], h32[:, :, :], h16[:, 0, :, :],
                                        ALU.subtract).then_inc(s_hlo, 1)

            def qk_lo(n, which):
                pool.wait_ge(s_qkhi, 2 * n + which + 1)
                nc.gpsimd.tensor_tensor(qk16[:, which, 1, :, :], qk32[:, :, :], qk16[:, which, 0, :, :],
                                        ALU.subtract).then_inc(s_qklo, 1)

            def o_lo(k):
                g, qb = divmod(k, QB)
                at = slice(2 * P * qb, 2 * P * qb + 2 * P)
                pool.wait_ge(s_ohi, k + 1)
                nc.gpsimd.tensor_tensor(o16[:, 1, g, at], o32[:, :], o16[:, 0, g, at],
                                        ALU.subtract).then_inc(s_olo, 1)

            def x_bias(j):
                n = 4 + j
                pool.wait_ge(s_x[n % 2], 16 * (n // 2 + 1))
                for t in range(2):
                    op = nc.gpsimd.tensor_tensor(x_in[:, n % 2, t, :], x_in[:, n % 2, t, :], bias_o[:, :], ALU.add)
                op.then_inc(s_xbias, 1)

            def front(s):
                if (n := front_pair(s, 1)) is not None:
                    inverse_deviation(n)
                if (n := front_pair(s, 3)) is not None:
                    h_lo(n)
                if (n := front_pair(s, 6)) is not None:
                    qk_lo(n, 0)
                if (n := front_pair(s, 7)) is not None:
                    qk_lo(n, 1)

            def end_round(totals):
                pool.wait_ge(s_arrive, 4)
                for name, value in totals.items():
                    pool.wait_ge(data_sems[name], value)
                for name in totals:
                    pool.sem_clear(data_sems[name])
                pool.sem_clear(s_arrive)
                for s in go.values():
                    pool.sem_inc(s, 1)

            nc.gpsimd.memset(minus_half[:, :], -0.5).then_inc(s_half, 1)
            pool.wait_ge(s_half, 1)
            for s in range(40):
                front(s)
            end_round(SETUP_TOTALS)

            with pool.Fori(0, B):
                for s in range(STEPS):
                    front(s)
                    if (k := block_at(s, -5)) is not None:
                        repeat_inverse(k)
                    if (k := block_at(s, 1)) is not None:
                        o_lo(k)
                    if (j := tail_pair(s, 2)) is not None:
                        x_bias(j)
                    if (j := tail_pair(s, 3)) is not None:
                        inverse_deviation(4 + j)
                    if (j := tail_pair(s, 5)) is not None:
                        h_lo(4 + j)
                end_round(ROUND_TOTALS)


def kernel(x, adj, L0_gnn_Wq, L0_gnn_bq, L0_gnn_Wk, L0_gnn_bk, L0_gnn_Wv, L0_gnn_bv, L0_gnn_Wo, L0_gnn_bo,
           L1_gnn_W, L1_gnn_b):
    import numpy as np
    import concourse.bacc as bacc
    from concourse.bass_utils import run_bass_kernel_spmd

    W = np.asarray(L1_gnn_W)
    w_t = np.concatenate([np.asarray(w).T for w in (L0_gnn_Wq, L0_gnn_Wk, L0_gnn_Wv, L0_gnn_Wo, W[:, :D], W[:, D:])],
                         axis=1)
    b_qk = np.stack([np.asarray(L0_gnn_bq).reshape(KC, P), np.asarray(L0_gnn_bk).reshape(KC, P)]).transpose(2, 0, 1)
    arrays = {
        "in_x": x, "in_adj": adj, "in_w_t": w_t, "in_b_qk": b_qk,
        "in_b_v": np.asarray(L0_gnn_bv)[None], "in_b_o": np.asarray(L0_gnn_bo)[None],
        "in_b_msg": np.asarray(L1_gnn_b)[None], "in_ident": np.eye(P, dtype=np.float32),
    }
    arrays = {n: np.ascontiguousarray(a) for n, a in arrays.items()}
    nc = bacc.Bacc("TRN2", target_bir_lowering=False, num_devices=1)
    args = [nc.dram_tensor(n, a.shape, mybir.dt.from_np(a.dtype), kind="ExternalInput").ap()
            for n, a in arrays.items()]
    qk_dram = nc.dram_tensor("qk_next", (2, 2, KC, P, N), F16, kind="Internal").ap()
    v_dram = nc.dram_tensor("v_next", (N, D), F32, kind="Internal").ap()
    result = nc.dram_tensor("out", (B, N, D), F32, kind="ExternalOutput").ap()
    gnn_kernel(nc, *args, qk_dram, v_dram, result)
    r = run_bass_kernel_spmd(nc, [arrays], core_ids=[0])
    return r.results[0]["out"]
```

```python
from contextlib import ExitStack

import concourse.bass as bass
from concourse import mybir

F32 = mybir.dt.float32
F16 = mybir.dt.float16
F8 = mybir.dt.float8e4
BF16 = mybir.dt.bfloat16
I32 = mybir.dt.int32
ALU = mybir.AluOpType
ACT = mybir.ActivationFunctionType

B, N, D = 8, 1024, 256
HEADS, DH = 8, 32
P = 128
NT = N // P
KC = D // P
GH = P // DH
QB = 4
QK_DMAS = 2 * 4
UNITS = HEADS * NT
BLOCKS = UNITS // 8
W_SCALE = 64.0
SCALE = float(DH) ** -0.5
EPS = 1e-5
NEG = -1e30
WQ, WK, WV, WO, WI = 0, D, 2 * D, 3 * D, 4 * D
W_COLS = 6 * D
TERMS = [(0, 0), (0, 1), (1, 0)]


def unit(u):
    return (u // 8) % 2, u // 16, (u // 2) % GH, u % 2


FRONT = ((17, 18, 20, 22), (27, 30, 33, 37), (43, 45, 49, 50), (52, 53, 54, 55))
TAIL = (31, 47, 1, 15)
SUMS = (28, 29, 32, 34, 35, 36, 38, 39)
PV = (10, 11, 12, 13, 14, 15, 15, 16)
FRONT_ALONE = tuple(tuple(8 + 4 * n + i for i in range(4)) for n in range(4))
TAIL_ALONE = (None, None, 1, 5)
SUMS_ALONE = tuple(range(17, 25))
PV_ALONE = (10, 10, 10, 10, 11, 11, 11, 11)
ADJ = (3, 4, 5, 6, 7, 11, 15, 19)
WEIGHTS = 2
ARRIVE, CLEAR = 21, 24


class Plan:

    def __init__(self, prev, own, front, front_steps=FRONT, tail_steps=TAIL, sums=SUMS, last_pv=PV, steps=UNITS):
        self.prev, self.own, self.front = prev, own, front
        self.front_steps, self.tail_steps, self.last_pv, self.steps = front_steps, tail_steps, last_pv, steps
        self.relus, self.split = ((-4, -3), -2) if own else ((-4, -4), -3)
        self.tails = [2, 3] * prev + [0, 1] * own
        fronts = range(4) if front else ()
        self.norms = sorted([("front", n) for n in fronts] + [("tail", m) for m in self.tails], key=self.turn_step)
        pieces = [(self.turn_step(j), "h", j) for j in self.norms]
        for n in fronts:
            pieces += [(at, kind, n) for at, kind in zip(front_steps[n][1:], "qkv")]
        for m in self.tails:
            pieces += [(tail_steps[m], "o", m), (tail_steps[m] + 10, "m", 2 * m), (tail_steps[m] + 11, "m", 2 * m + 1)]
        if prev:
            pieces += [(s, "a", i) for i, s in enumerate(sums)]
        self.pieces = sorted(pieces, key=lambda p: p[0])
        assert len({p[0] for p in pieces}) == len(pieces) and self.pieces[-1][0] < steps - 3
        self.copies = [p[1:] for p in self.pieces if p[1] in "ma"]

    def turn_step(self, job):
        return self.front_steps[job[1]][0] if job[0] == "front" else self.tail_steps[job[1]] + 9

    def fill(self, kind, index):
        return [p[1:] for p in self.pieces].index((kind, index)) + 1

    def messages(self, tile):
        return [p[2] for p in self.pieces if p[1] == "m"].index(tile) + 1

    def piece_at(self, s, kind, offset=0):
        return [p[2] for p in self.pieces if p[0] == s - offset and p[1] == kind]

    def norms_at(self, s, offset):
        return [(i, j) for i, j in enumerate(self.norms) if self.turn_step(j) == s - offset]

    def exists(self, i):
        return self.prev if i < 0 else self.own

    def unit_at(self, s, offset=0):
        return [u for u in (s - offset,) if self.exists(u) and u < UNITS]

    def sums_at(self, s):
        return [k for k in range(-1, BLOCKS) if self.exists(k) and 8 * k + 9 == s]

    def pv_at(self, s, offset=0):
        found = []
        for k in range(-2, BLOCKS):
            tiles = [t for t in range(NT) if 8 * k + (self.last_pv if k == -1 else PV)[t] == s - offset]
            if self.exists(k) and tiles:
                found.append((k, tiles))
        return found

    def blocks_at(self, s, offset):
        return [k for k, tiles in self.pv_at(s, offset) if tiles[-1] == NT - 1]

    def totals(self):
        norms, tails = len(self.norms), len(self.tails)
        out = {"stats": 2 * norms, "moments": 2 * norms, "side": len(self.pieces),
               "x0": 16 * ((norms + 1) // 2), "x1": 16 * (norms // 2)}
        out |= {n: norms for n in ("vareps", "rstd", "negmean", "relu", "hhi", "hlo", "ht")}
        out |= {n: tails for n in ("xbias", "x1done")}
        out |= {n: 2 * tails for n in ("m32", "msghi", "msglo", "self", "scaled", "base")}
        if self.prev:
            out |= {"sum32": NT, "result": NT, "stored": 64}
        if self.own:
            out |= {n: UNITS for n in ("scores", "masked", "exp", "copy0", "copy1")}
            out |= {n: BLOCKS for n in ("pv", "invunit", "inv", "invtp", "invt", "o32", "ohi", "olo")}
            out |= {"tp": 2 * UNITS, "qk1": 16 * QK_DMAS, "vop0": 16, "vop1": 16}
        if self.front:
            out |= {"qk32": 8, "qkhi": 8, "qklo": 8, "v32": 4, "v": 4, "qkept": 64, "kkept": 64, "vkept": 64,
                    "qk0": 16 * QK_DMAS * (1 if self.own else 2)}
        return {n: v for n, v in out.items() if v}


class Round:

    def __init__(self, plan, now, was=None, before=None):
        self.plan, self.now, self.was, self.before = plan, now, was, before

    def known(self, name, n):
        return n > 0 or self.was is not None and name in self.before.totals()

    def count(self, name, n):
        if n > 0:
            return self.now[name], n
        return self.was[name], self.before.totals()[name] + n

    def of(self, i):
        return self.now if i >= 0 else self.was


def buffer(u):
    return 1 if u % UNITS == UNITS - 1 else u % UNITS % 3


def buffer_before(u):
    return {0: -4, 1: -1, 2: -2, UNITS - 1: UNITS - 3}.get(u, u - 3)


def gnn_kernel(nc, x, adj, w_t, b_qk, b_v, b_o, b_msg, ident, qk_dram, v_dram, out):
    with ExitStack() as ctx:
        def sb(name, shape, dt):
            return ctx.enter_context(nc.sbuf_tensor(name, shape, dt))

        def pb(name, shape, dt):
            return ctx.enter_context(nc.psum_tensor(name, shape, dt))

        ident32 = sb("ident32", [P, P], F32)
        ident16 = sb("ident16", [P, P], F16)
        w16 = sb("w16", [P, 2, KC, W_COLS], F16)
        bias_qk = sb("bias_qk", [P, 2, KC], F32)
        bias_v = sb("bias_v", [P, D], F32)
        bias_o = sb("bias_o", [P, D], F32)
        bias_msg = sb("bias_msg", [P, D], F32)
        minus_half = sb("minus_half", [P, 2], F32)
        mask_add = sb("mask_add", [P, NT, N], BF16)
        adj_t = sb("adj_t", [P, NT, N], F8)
        deg = sb("deg", [P, NT], F32)
        q_op = sb("q_op", [P, HEADS, N], F16)
        k_op = sb("k_op", [P, HEADS, N], F16)
        v_op = sb("v_op", [P, KC, NT, P], F32)
        qk16 = sb("qk16", [P, 2, 2, KC, 2 * P], F16)
        v32 = sb("v32", [P, 2, D], F32)
        probs = sb("probs", [P, 3, N], F32)
        probs_t = sb("probs_t", [P, 2, GH, NT, 2 * P], F32)
        neg_max = sb("neg_max", [P, UNITS], F32)
        row_sum = sb("row_sum", [P, UNITS], F32)
        inv_unit = sb("inv_unit", [P, 8], F32)
        inv_sum = sb("inv_sum", [P, 2, GH, DH], F32)
        o32 = sb("o32", [P, 2 * P], F32)
        o16 = sb("o16", [P, 2, KC, N], F16)
        x_in = sb("x_in", [P, 2, 2, D], F32)
        x1 = sb("x1", [P, 2, D], F32)
        stats = sb("stats", [P, 16, 6], F32)
        mean_var = sb("mean_var", [P, 16, 2], F32)
        var_eps = sb("var_eps", [P, 16], F32)
        rstd = sb("rstd", [P, 16], F32)
        neg_mean = sb("neg_mean", [P, 16], F32)
        h32 = sb("h32", [P, 2, D], F32)
        h16 = sb("h16", [P, 2, 2, D], F16)
        h_t = sb("h_t", [P, 2, KC, 2 * P], F16)
        qk32 = sb("qk32", [P, KC, 2 * P], F32)
        msg16 = sb("msg16", [P, NT, 2, D], F16)
        m32 = sb("m32", [P, 2, 2 * D], F32)
        base = sb("base", [P, NT, D], F32)

        adj_raw = probs_t[:, 0, :, :, :].bitcast(I32).rearrange("p h k q -> p (h k q)")\
                                        .rearrange("p (t n) -> p t n", t=NT)
        adj16 = probs_t[:, 1, 0, 0:4, :].bitcast(F16).rearrange("p k q -> p (k q)").rearrange("p (t n) -> p t n", t=2)
        w_raw = probs[:, :, :].rearrange("p a n -> p (a n)").rearrange("p (c n) -> p c n", c=KC)

        s_ps = pb("s_ps", [P, 2, N], F32)
        t_ps = pb("t_ps", [P, 2, 512], F32)
        o_ps = pb("o_ps", [P, 512], F32)
        side_ps = pb("side_ps", [P, 512], F32)

        sems = {}

        def sem(name):
            sems[name] = ctx.enter_context(nc.semaphore(name))
            return sems[name]

        s_ident = sem("s_ident")
        s_const = sem("s_const")
        s_wload = sem("s_wload")
        s_adjload = [sem(f"s_adjload{t}") for t in range(NT)]
        s_id16 = sem("s_id16")
        s_biases = sem("s_biases")
        s_half = sem("s_half")
        s_whi = sem("s_whi")
        s_wlo = sem("s_wlo")
        s_adj16 = sem("s_adj16")
        s_mask = sem("s_mask")
        s_adjtp = sem("s_adjtp")
        s_adjt = sem("s_adjt")
        round_sems = (
            "scores",
            "masked",
            "exp",
            "tp",
            "copy0",
            "copy1",
            "pv",
            "invunit",
            "inv",
            "invtp",
            "invt",
            "o32",
            "ohi",
            "olo",
            "x0", "x1",
            "stats",
            "moments",
            "vareps",
            "rstd",
            "negmean",
            "relu",
            "hhi",
            "hlo",
            "side",
            "ht",
            "qk32",
            "qkhi",
            "qklo",
            "v32",
            "v",
            "qkept", "kkept",
            "vkept",
            "xbias",
            "x1done",
            "m32",
            "msghi",
            "msglo",
            "self",
            "scaled",
            "base",
            "sum32",
            "result",
            "stored",
            "qk0",
            "qk1",
            "vop0", "vop1",
        )
        sets = [{name: sem(f"s_{name}_{i}") for name in round_sems} for i in range(2)]
        s_arrive = sem("s_arrive")
        go = {e: sem(f"s_go_{e}") for e in ("pe", "act", "dve", "sp")}

        def x1_of(plan, m):
            return x1 if plan.own or m == 2 else v32

        def h_lo(eng, r, order):
            eng.wait_ge(r.now["hhi"], order + 1)
            eng.tensor_tensor(h16[:, 1, :, :], h32[:, :, :], h16[:, 0, :, :],
                              ALU.subtract).then_inc(r.now["hlo"], 1)

        def qk_lo(eng, r, n, which):
            eng.wait_ge(r.now["qkhi"], 2 * n + which + 1)
            eng.tensor_tensor(qk16[:, which, 1, :, :], qk32[:, :, :], qk16[:, which, 0, :, :],
                              ALU.subtract).then_inc(r.now["qklo"], 1)

        def o_lo(eng, r, k):
            at = slice(2 * P * (k % BLOCKS // 2), 2 * P * (k % BLOCKS // 2) + 2 * P)
            eng.wait_ge(*r.count("ohi", k + 1))
            eng.tensor_tensor(o16[:, 1, k % 2, at], o32[:, :], o16[:, 0, k % 2, at],
                              ALU.subtract).then_inc(r.of(k)["olo"], 1)

        def message_lo(eng, r, tile):
            copy = m32[:, r.plan.copies.index(("m", tile)) % 2, :]
            eng.wait_ge(r.now["msghi"], r.plan.messages(tile))
            eng.tensor_tensor(msg16[:, tile, 1, :], copy[:, D:2 * D], msg16[:, tile, 0, :],
                              ALU.subtract).then_inc(r.now["msglo"], 1)

        def own_terms(eng, r, tile):
            i = r.plan.messages(tile)
            copy = m32[:, r.plan.copies.index(("m", tile)) % 2, 0:D]
            eng.wait_ge(r.now["m32"], i)
            eng.tensor_tensor(copy, copy, bias_msg[:, :], ALU.add).then_inc(r.now["self"], 1)
            eng.wait_ge(r.now["self"], i)
            eng.tensor_scalar(copy, copy, deg[:, tile:tile + 1], 1.0 / W_SCALE, ALU.mult,
                              ALU.mult).then_inc(r.now["scaled"], 1)
            eng.wait_ge(r.now["scaled"], i)
            if r.plan.prev and tile == 0:
                eng.wait_ge(r.now["stored"], 64)
            eng.tensor_tensor(base[:, tile, :], copy, x1_of(r.plan, tile // 2)[:, tile % 2, :],
                              ALU.add).then_inc(r.now["base"], 1)

        def side_bank(plan, kind, index):
            return side_ps if plan.own or plan.fill(kind, index) % 2 == 0 else s_ps[:, 1, 512:1024]

        x_t = x.rearrange("b (t p) c -> b p t c", p=P)
        out_t = out.rearrange("b (t p) c -> b p t c", p=P)
        qk_rows = [qk_dram[which].rearrange("a g p n -> p (a g) n") for which in range(2)]
        v_rows = v_dram.rearrange("(t p) c -> p t c", p=P)

        front_only = Plan(prev=False, own=False, front=True, front_steps=FRONT_ALONE, steps=40)
        middle = Plan(prev=True, own=True, front=True)
        last = Plan(prev=True, own=True, front=False)
        SETUP = Round(front_only, sets[1])
        FIRST = Round(Plan(prev=False, own=True, front=True), sets[0], sets[1], front_only)
        MIDDLE = [Round(middle, sets[b], sets[1 - b], middle) for b in range(2)]
        LAST = Round(last, sets[1], sets[0], middle)
        REST = Round(Plan(prev=True, own=False, front=False, tail_steps=TAIL_ALONE, sums=SUMS_ALONE,
                          last_pv=PV_ALONE, steps=40), sets[0], sets[1], last)

        def arrive(eng):
            eng.sem_inc(s_arrive, 1)

        def let_go(eng, name):
            eng.wait_ge(go[name], 1)
            eng.sem_clear(go[name])

        block = ctx.enter_context(nc.Block())

        @block.sync
        def _(sp):
            def load_x(r, i, b):
                kind, n = r.plan.norms[i]
                plan, place = (r.plan, i - 2) if i >= 2 else (r.before, i - 2)
                if plan:
                    before, m = plan.norms[place]
                    if before == "front":
                        sp.wait_ge(*r.count("relu", i - 1))
                    else:
                        done = plan.tails.index(m) + 1 - (0 if i >= 2 else len(plan.tails))
                        sp.wait_ge(*r.count("x1done", done))
                batch = b + 1 if kind == "front" else (b - 1 if n >= 2 else b)
                sp.dma_start(x_in[:, i % 2, :, :],
                             x_t[bass.ds(batch, 1), :, 2 * n:2 * n + 2, :].rearrange("b p t c -> p (b t) c")
                             ).then_inc(r.now[("x0", "x1")[i % 2]], 16)

            def keep_qk(r, n, which):
                if n == 0 and r.plan.own:
                    sp.wait_ge(r.now["qk1"], 16 * QK_DMAS)
                sp.wait_ge(r.now["qklo"], 2 * n + which + 1)
                sp.dma_start(qk_rows[which][:, :, 2 * P * n:2 * P * n + 2 * P],
                             qk16[:, which, :, :, :].rearrange("p a g n -> p (a g) n")
                             ).then_inc(r.now[("qkept", "kkept")[which]], 16)

            def keep_v(r, n):
                if n == 0 and r.plan.own:
                    sp.wait_ge(r.now["vop0"], 16)
                    sp.wait_ge(r.now["vop1"], 16)
                sp.wait_ge(r.now["v"], n + 1)
                sp.dma_start(v_rows[:, 2 * n:2 * n + 2, :], v32[:, :, :]).then_inc(r.now["vkept"], 16)

            def load_qk(r, g, done, nodes=slice(0, N)):
                for rows, (q_part, k_part) in enumerate([(0, 0), (0, 1), (1, 0), (1, 1)]):
                    for which, part, to in ((0, q_part, q_op), (1, k_part, k_op)):
                        sp.dma_start(to[DH * rows:DH * rows + DH, GH * g:GH * g + GH, nodes],
                                     qk_dram[which, part, g].rearrange("(h p) n -> p h n", p=DH)[:, :, nodes]
                                     ).then_inc(done, 16)

            def load_v(r, g):
                sp.wait_ge(*r.count("vkept", 0))
                if r.known("pv", g - 1):
                    sp.wait_ge(*r.count("pv", g - 1))
                sp.dma_start(v_op[:, g, :, :], v_rows[:, :, P * g:P * g + P]).then_inc(r.now[("vop0", "vop1")[g]], 16)

            def store(r, i, b):
                sp.wait_ge(r.now["result"], 2 * i + 2)
                sp.dma_start(out_t[bass.ds(b - 1, 1), :, 2 * i:2 * i + 2, :].rearrange("b p t c -> p (b t) c"),
                             base[:, 2 * i:2 * i + 2, :]).then_inc(r.now["stored"], 16)

            def a_round(r, b):
                for i in range(0 if r is SETUP else 2):
                    load_x(r, i, b)
                if r.plan.own:
                    if r.known("scores", 0):
                        sp.wait_ge(*r.count("scores", 0))
                    load_qk(r, 1, r.now["qk1"])
                for s in range(r.plan.steps):
                    for g in range(KC):
                        if r.plan.own and s == PV[-1] - 16 + 8 * g + 1:
                            load_v(r, g)
                    for i, _ in r.plan.norms_at(s, -2):
                        if i + 2 < len(r.plan.norms):
                            load_x(r, i + 2, b)
                    for n in r.plan.piece_at(s, "q", 2):
                        keep_qk(r, n, 0)
                    for n in r.plan.piece_at(s, "k", 2):
                        keep_qk(r, n, 1)
                    for n in r.plan.piece_at(s, "v", 2):
                        keep_v(r, n)
                    if r is SETUP and s == FRONT_ALONE[1][3] + 2:
                        sp.wait_ge(r.now["qkept"], 32)
                        sp.wait_ge(r.now["kkept"], 32)
                        load_qk(r, 0, r.now["qk0"], slice(0, N // 2))
                    for i in r.plan.piece_at(s, "a", 2):
                        if i % 2:
                            store(r, i // 2, b)
                    if r.was and s == ARRIVE:
                        arrive(sp)
                if r.plan.front:
                    sp.wait_ge(r.now["qkept"], 64)
                    sp.wait_ge(r.now["kkept"], 64)
                    if r.plan.own:
                        sp.wait_ge(r.now["scores"], UNITS - 8)
                    load_qk(r, 0, r.now["qk0"], slice(N // 2 if r is SETUP else 0, N))
                if r.was:
                    let_go(sp, "sp")

            sp.dma_start(ident32[:, :], ident).then_inc(s_ident, 16)
            for i in range(2):
                load_x(SETUP, i, -1)
            sp.dma_start(w_raw, w_t.rearrange("(c p) n -> p c n", p=P)).then_inc(s_wload, 16)
            for t in range(NT):
                sp.dma_start(adj_raw[:, t, :], adj[P * t:P * t + P, :]).then_inc(s_adjload[t], 16)
                if t == 1:
                    sp.dma_start(bias_qk[:, :, :], b_qk).then_inc(s_const, 16)
                    for to, of in ((bias_v, b_v), (bias_o, b_o), (bias_msg, b_msg)):
                        sp.dma_start(to[:, :], of.to_broadcast([P, D])).then_inc(s_const, 16)
            a_round(SETUP, -1)
            a_round(FIRST, 0)
            with sp.Fori(0, (B - 2) // 2) as i:
                a_round(MIDDLE[1], 2 * i + 1)
                a_round(MIDDLE[0], 2 * i + 2)
            a_round(LAST, B - 1)
            a_round(REST, B)

        @block.tensor
        def _(pe):
            def adj_transposes(t):
                pe.wait_ge(s_adj16, t + 1)
                if t >= 2:
                    pe.wait_ge(s_adjt, t - 1)
                bank = t_ps[:, t % 2, :].bitcast(F16)
                for j in range(NT):
                    mm = pe.transpose(bank[:, P * j:P * j + P], adj16[:, t % 2, P * j:P * j + P], ident16[:, :])
                mm.then_inc(s_adjtp, 1)

            def scores(r, u):
                g, qb, hh, qt = unit(u)
                if r.known("masked", u - 1):
                    pe.wait_ge(*r.count("masked", u - 1))
                if u == 0:
                    pe.wait_ge(*r.count("qk0", 0))
                if u == 8:
                    pe.wait_ge(r.now["qk1"], 16 * QK_DMAS)
                h = GH * g + hh
                at = (2 * qb + qt) * P
                for c in range(2):
                    mm = pe.matmul(s_ps[:, u % 2, 512 * c:512 * c + 512], q_op[:, h, at:at + P],
                                   k_op[:, h, 512 * c:512 * c + 512], start=True, stop=True)
                mm.then_inc(r.now["scores"], 1)

            def transposes(r, u):
                pe.wait_ge(*r.count("exp", u + 1))
                for half in range(2):
                    if r.known("copy0", u):
                        pe.wait_ge(*r.count(("copy0", "copy1")[half], u))
                    for j in range(4):
                        k = 4 * half + j
                        mm = pe.transpose(t_ps[:, half, P * j:P * j + P], probs[:, buffer(u), P * k:P * k + P],
                                          ident32[:, :])
                    mm.then_inc(r.of(u)["tp"], 1)

            def times_v(r, k, tiles):
                g = k % 2
                if tiles[0] == 0:
                    pe.wait_ge(*r.count("copy0", 8 * k + 8))
                    pe.wait_ge(*r.count("copy1", 8 * k + 8))
                    if r.known("o32", k):
                        pe.wait_ge(*r.count("o32", k))
                    if k in (0, 1):
                        pe.wait_ge(r.now[("vop0", "vop1")[g]], 16)
                for t in tiles:
                    for hh in range(GH):
                        at = slice(DH * hh, DH * hh + DH)
                        mm = pe.matmul(o_ps[at, 0:2 * P], v_op[:, g, t, at], probs_t[:, k % 2, hh, t, :],
                                       start=(t == 0), stop=(t == NT - 1))
                if tiles[-1] == NT - 1:
                    mm.then_inc(r.of(k)["pv"], 1)

            def turn_inverse(r, k):
                pe.wait_ge(*r.count("inv", k + 1))
                for qt in range(2):
                    mm = pe.transpose(o_ps[:, 2 * P + P * qt:2 * P + P * qt + P],
                                      inv_sum[:, qt, :, :].rearrange("p h d -> p (h d)"), ident32[:, :])
                mm.then_inc(r.of(k)["invtp"], 1)

            def bank_read(r, kind, index):
                at = r.plan.fill(kind, index) - (1 if r.plan.own else 2)
                if at < 0:
                    return
                if at == 0:
                    if r.was:
                        pe.wait_ge(*r.count("v32" if r.before.front else "m32", 0))
                    return
                _, before, i = r.plan.pieces[at - 1]
                if before == "h":
                    pe.wait_ge(r.now["ht"], r.plan.norms.index(i) + 1)
                elif before in "qk":
                    pe.wait_ge(r.now["qk32"], 2 * i + (2 if before == "k" else 1))
                elif before == "v":
                    pe.wait_ge(r.now["v32"], i + 1)
                elif before == "o":
                    pe.wait_ge(r.now["x1done"], r.plan.tails.index(i) + 1)
                elif before == "m":
                    pe.wait_ge(r.now["m32"], r.plan.messages(i))
                else:
                    pe.wait_ge(r.now["sum32"], i + 1)

            def turn_h(r, order, job):
                pe.wait_ge(r.now["hhi"], order + 1)
                pe.wait_ge(r.now["hlo"], order + 1)
                bank_read(r, "h", job)
                bank = side_bank(r.plan, "h", job)[:, :].bitcast(F16).rearrange("p (a c n) -> p a c n", a=2, c=KC)
                for part in range(2):
                    for c in range(KC):
                        for t in range(2):
                            mm = pe.transpose(bank[:, part, c, P * t:P * t + P], h16[:, part, t, P * c:P * c + P],
                                              ident16[:, :])
                mm.then_inc(r.now["side"], 1)

            def q_or_k(r, n, which):
                bank = side_bank(r.plan, "qk"[which], n)
                if r is SETUP and n + which == 0:
                    pe.wait_ge(s_whi, 1)
                    pe.wait_ge(s_wlo, 1)
                if which == 0:
                    pe.wait_ge(r.now["ht"], r.plan.norms.index(("front", n)) + 1)
                bank_read(r, "qk"[which], n)
                for g in range(KC):
                    col = (WQ, WK)[which] + P * g
                    for i, (w_part, h_part) in enumerate(TERMS):
                        for c in range(KC):
                            mm = pe.matmul(bank[:, 2 * P * g:2 * P * g + 2 * P], w16[:, w_part, c, col:col + P],
                                           h_t[:, h_part, c, :], start=(i + c == 0), stop=(i == 2 and c == KC - 1))
                mm.then_inc(r.now["side"], 1)

            def v_pair(r, n):
                bank = side_bank(r.plan, "v", n)
                bank_read(r, "v", n)
                for t in range(2):
                    for i, (h_part, w_part) in enumerate(TERMS):
                        for c in range(KC):
                            mm = pe.matmul(bank[:, D * t:D * t + D], h_t[:, h_part, c, P * t:P * t + P],
                                           w16[:, w_part, c, WV:WV + D], start=(i + c == 0),
                                           stop=(i == 2 and c == KC - 1))
                mm.then_inc(r.now["side"], 1)

            def output_product(r, m):
                bank = side_bank(r.plan, "o", m)
                done = 2 * m + 2 - (BLOCKS if m >= 2 else 0)
                pe.wait_ge(*r.count("ohi", done))
                pe.wait_ge(*r.count("olo", done))
                bank_read(r, "o", m)
                for t in range(2):
                    at = (2 * m + t) * P
                    for i, (o_part, w_part) in enumerate(TERMS):
                        for c in range(KC):
                            mm = pe.matmul(bank[:, D * t:D * t + D], o16[:, o_part, c, at:at + P],
                                           w16[:, w_part, c, WO:WO + D], start=(i + c == 0),
                                           stop=(i == 2 and c == KC - 1))
                mm.then_inc(r.now["side"], 1)

            def messages(r, tile):
                bank = side_bank(r.plan, "m", tile)
                if tile % 2 == 0:
                    pe.wait_ge(r.now["ht"], r.plan.norms.index(("tail", tile // 2)) + 1)
                bank_read(r, "m", tile)
                at = P * (tile % 2)
                for i, (h_part, w_part) in enumerate(TERMS):
                    for c in range(KC):
                        mm = pe.matmul(bank[:, :], h_t[:, h_part, c, at:at + P], w16[:, w_part, c, WI:WI + 2 * D],
                                       start=(i + c == 0), stop=(i == 2 and c == KC - 1))
                mm.then_inc(r.now["side"], 1)

            def neighbour_sums(r, i):
                bank = side_bank(r.plan, "a", i)
                bank_read(r, "a", i)
                for j in range(NT):
                    if i == 0 and j >= NT // 2:
                        pe.wait_ge(r.now["msghi"], r.plan.messages(j))
                        pe.wait_ge(r.now["msglo"], r.plan.messages(j))
                    for part in range(2):
                        mm = pe.matmul(bank[:, 0:D], adj_t[:, j, P * i:P * i + P], msg16[:, j, part, :],
                                       start=(j + part == 0), stop=(j == NT - 1 and part == 1))
                mm.then_inc(r.now["side"], 1)

            def side(r, s):
                for order, job in r.plan.norms_at(s, 0):
                    turn_h(r, order, job)
                for n in r.plan.piece_at(s, "q"):
                    q_or_k(r, n, 0)
                for n in r.plan.piece_at(s, "k"):
                    q_or_k(r, n, 1)
                for n in r.plan.piece_at(s, "v"):
                    v_pair(r, n)
                for m in r.plan.piece_at(s, "o"):
                    output_product(r, m)
                for tile in r.plan.piece_at(s, "m"):
                    messages(r, tile)
                for i in r.plan.piece_at(s, "a"):
                    neighbour_sums(r, i)

            def a_round(r):
                for s in range(r.plan.steps):
                    if r.plan.own:
                        scores(r, s)
                    for u in r.plan.unit_at(s, 2):
                        transposes(r, u)
                    for k, tiles in r.plan.pv_at(s):
                        times_v(r, k, tiles)
                    for k in r.plan.blocks_at(s, 0):
                        turn_inverse(r, k)
                    side(r, s)
                    if r is SETUP and s - 1 in ADJ:
                        adj_transposes(ADJ.index(s - 1))
                    if r.was and s == ARRIVE:
                        arrive(pe)
                if r.was:
                    let_go(pe, "pe")

            pe.wait_ge(s_id16, 1)
            a_round(SETUP)
            a_round(FIRST)
            with pe.Fori(0, (B - 2) // 2):
                a_round(MIDDLE[1])
                a_round(MIDDLE[0])
            a_round(LAST)
            a_round(REST)

        @block.scalar
        def _(act):
            def adj_float(t):
                act.wait_ge(s_adjload[t], 16)
                if t >= 2:
                    act.wait_ge(s_adjtp, t - 1)
                nc.scalar.activation(adj16[:, t % 2, :], adj_raw[:, t, :], ACT.Copy,
                                     accum_out=deg[:, t:t + 1]).then_inc(s_adj16, 1)

            def weight_hi():
                act.wait_ge(s_wload, 16)
                nc.scalar.activation(w16[:, 0, :, :], w_raw, ACT.Copy, scale=W_SCALE).then_inc(s_whi, 1)

            def exponentials(r, u):
                act.wait_ge(r.now["masked"], u + 1)
                at = probs[:, buffer(u), :]
                nc.scalar.activation(at, at, ACT.Exp, bias=neg_max[:, u:u + 1], scale=-1.0,
                                     accum_out=row_sum[:, u:u + 1]).then_inc(r.now["exp"], 1)

            def copy_half(r, u):
                _, _, hh, qt = unit(u % UNITS)
                act.wait_ge(*r.count("tp", 2 * u + 1))
                nc.scalar.copy(probs_t[:, u // 8 % 2, hh, 0:4, P * qt:P * qt + P],
                               t_ps[:, 0, :].rearrange("p (k q) -> p k q", k=4)).then_inc(r.of(u)["copy0"], 1)

            def copy_inverse(r, k):
                act.wait_ge(*r.count("invtp", k + 1))
                if r.known("ohi", k):
                    act.wait_ge(*r.count("ohi", k))
                    act.wait_ge(*r.count("olo", k))
                nc.scalar.copy(o32[:, :], o_ps[:, 2 * P:4 * P]).then_inc(r.of(k)["invt"], 1)

            def relu(r, order, job, t):
                if t == 0:
                    act.wait_ge(r.now["negmean"], order + 1)
                    if r.known("hhi", order):
                        act.wait_ge(*r.count("hhi", order))
                        act.wait_ge(*r.count("hlo", order))
                source = x_in[:, order % 2, :, :] if job[0] == "front" else x1_of(r.plan, job[1])[:, :, :]
                i = 2 * order + t
                op = nc.scalar.activation(h32[:, t, :], source[:, t, :], ACT.Relu, bias=neg_mean[:, i:i + 1],
                                          scale=rstd[:, i:i + 1])
                if t == 1:
                    op.then_inc(r.now["relu"], 1)

            def copy_h_t(r, job):
                act.wait_ge(r.now["side"], r.plan.fill("h", job))
                nc.scalar.copy(h_t[:, :, :, :].rearrange("p a c n -> p (a c n)"),
                               side_bank(r.plan, "h", job)[:, :].bitcast(F16)).then_inc(r.now["ht"], 1)

            def copy_qk(r, n, which):
                bank = side_bank(r.plan, "qk"[which], n)
                act.wait_ge(r.now["side"], r.plan.fill("qk"[which], n))
                if r.known("qkhi", 2 * n + which):
                    act.wait_ge(*r.count("qkhi", 2 * n + which))
                    act.wait_ge(*r.count("qklo", 2 * n + which))
                if r is SETUP and n + which == 0:
                    act.wait_ge(s_biases, 2)
                for g in range(KC):
                    op = nc.scalar.activation(qk32[:, g, :], bank[:, 2 * P * g:2 * P * g + 2 * P],
                                              ACT.Identity, bias=bias_qk[:, which, g:g + 1],
                                              scale=(SCALE if which == 0 else 1.0) / W_SCALE)
                op.then_inc(r.now["qk32"], 1)

            def copy_v(r, n):
                bank = side_bank(r.plan, "v", n)
                act.wait_ge(r.now["side"], r.plan.fill("v", n))
                if r.known("vkept", n):
                    act.wait_ge(*r.count("vkept", 16 * n))
                nc.scalar.activation(v32[:, :, :].rearrange("p t c -> p (t c)"), bank[:, :], ACT.Copy,
                                     scale=1.0 / W_SCALE).then_inc(r.now["v32"], 1)

            def copy_buffer_free(r, use):
                if use < 2:
                    if r.known("base", 0):
                        act.wait_ge(*r.count("base", use - 1))
                        act.wait_ge(*r.count("msglo", use - 1))
                    return
                kind, i = r.plan.copies[use - 2]
                if kind == "m":
                    act.wait_ge(r.now["base"], r.plan.messages(i))
                    act.wait_ge(r.now["msglo"], r.plan.messages(i))
                else:
                    act.wait_ge(r.now["result"], i + 1)

            def copy_messages(r, tile):
                bank = side_bank(r.plan, "m", tile)
                use = r.plan.copies.index(("m", tile))
                act.wait_ge(r.now["side"], r.plan.fill("m", tile))
                copy_buffer_free(r, use)
                nc.scalar.copy(m32[:, use % 2, :], bank[:, :]).then_inc(r.now["m32"], 1)

            def copy_sums(r, i):
                bank = side_bank(r.plan, "a", i)
                use = r.plan.copies.index(("a", i))
                act.wait_ge(r.now["side"], r.plan.fill("a", i))
                copy_buffer_free(r, use)
                nc.scalar.activation(m32[:, use % 2, 0:D], bank[:, 0:D], ACT.Copy,
                                     scale=1.0 / W_SCALE).then_inc(r.now["sum32"], 1)

            def side(r, s):
                for _, job in r.plan.norms_at(s, 0):
                    copy_h_t(r, job)
                for n in r.plan.piece_at(s, "q"):
                    copy_qk(r, n, 0)
                for n in r.plan.piece_at(s, "k"):
                    copy_qk(r, n, 1)
                for n in r.plan.piece_at(s, "v"):
                    copy_v(r, n)
                for tile in r.plan.piece_at(s, "m"):
                    copy_messages(r, tile)
                for i in r.plan.piece_at(s, "a"):
                    copy_sums(r, i)
                for t in range(2):
                    for order, job in r.plan.norms_at(s, r.plan.relus[t]):
                        relu(r, order, job, t)

            def a_round(r):
                for s in range(r.plan.steps):
                    for u in r.plan.unit_at(s, 2):
                        copy_half(r, u)
                    for k in r.plan.blocks_at(s, 1):
                        copy_inverse(r, k)
                    if r.plan.own:
                        exponentials(r, s)
                    if r is SETUP and s == WEIGHTS:
                        weight_hi()
                    if r is SETUP and s in ADJ:
                        adj_float(ADJ.index(s))
                    side(r, s)
                    if r.was and s == ARRIVE:
                        arrive(act)
                if r.was:
                    let_go(act, "act")

            a_round(SETUP)
            a_round(FIRST)
            with act.Fori(0, (B - 2) // 2):
                a_round(MIDDLE[1])
                a_round(MIDDLE[0])
            a_round(LAST)
            a_round(REST)

        @block.vector
        def _(dve):
            def adj_masks(t):
                dve.wait_ge(s_adjload[t], 16)
                nc.vector.tensor_scalar(mask_add[:, t, :], adj_raw[:, t, :], 0.0, NEG, ALU.is_equal,
                                        ALU.mult).then_inc(s_mask, 1)
                dve.wait_ge(s_adjtp, t + 1)
                nc.vector.tensor_copy(adj_t[:, :, P * t:P * t + P],
                                      t_ps[:, t % 2, :].bitcast(F16).rearrange("p (j q) -> p j q", j=NT),
                                      saturate=False).then_inc(s_adjt, 1)

            def weight_lo():
                dve.wait_ge(s_whi, 1)
                nc.vector.scalar_tensor_tensor(out=w16[:, 1, :, :], in0=w_raw, scalar=W_SCALE, in1=w16[:, 0, :, :],
                                               op0=ALU.mult, op1=ALU.subtract).then_inc(s_wlo, 1)
                dve.wait_ge(s_const, 16 * 4)
                nc.vector.tensor_scalar(bias_qk[:, 0, :], bias_qk[:, 0, :], SCALE, None, ALU.mult).then_inc(s_biases, 1)
                nc.vector.tensor_scalar(bias_msg[:, :], bias_msg[:, :], W_SCALE, None, ALU.mult).then_inc(s_biases, 1)

            def mask_scores(r, u):
                _, qb, _, qt = unit(u)
                dve.wait_ge(r.now["scores"], u + 1)
                before = buffer_before(u)
                if r.known("tp", before + 1):
                    dve.wait_ge(*r.count("tp", 2 * before + 2))
                nc.vector.tensor_tensor_reduce(
                    out=probs[:, buffer(u), :], in0=s_ps[:, u % 2, :], in1=mask_add[:, 2 * qb + qt, :], scale=-1.0,
                    scalar=3e38, op0=ALU.add, op1=ALU.min, accum_out=neg_max[:, u:u + 1]).then_inc(r.now["masked"], 1)

            def copy_half(r, u):
                _, _, hh, qt = unit(u % UNITS)
                dve.wait_ge(*r.count("tp", 2 * u + 2))
                nc.vector.tensor_copy(probs_t[:, u // 8 % 2, hh, 4:8, P * qt:P * qt + P],
                                      t_ps[:, 1, :].rearrange("p (k q) -> p k q", k=4)).then_inc(r.of(u)["copy1"], 1)

            def inverse_sums(r, k):
                dve.wait_ge(*r.count("exp", 8 * k + 8))
                if r.known("inv", k):
                    dve.wait_ge(*r.count("inv", k))
                at = 8 * (k % BLOCKS)
                nc.vector.reciprocal(inv_unit[:, :], row_sum[:, at:at + 8]).then_inc(r.of(k)["invunit"], 1)

            def normalise(r, k):
                at = slice(2 * P * (k % BLOCKS // 2), 2 * P * (k % BLOCKS // 2) + 2 * P)
                dve.wait_ge(*r.count("invt", k + 1))
                nc.vector.tensor_tensor(o32[:, :], o_ps[:, 0:2 * P], o32[:, :], ALU.mult).then_inc(r.of(k)["o32"], 1)
                dve.wait_ge(*r.count("o32", k + 1))
                nc.vector.tensor_copy(o16[:, 0, k % 2, at], o32[:, :]).then_inc(r.of(k)["ohi"], 1)

            def statistics(r, order, job):
                if job[0] == "front":
                    dve.wait_ge(r.now[("x0", "x1")[order % 2]], 16 * (order // 2 + 1))
                source = x_in[:, order % 2, :, :] if job[0] == "front" else x1_of(r.plan, job[1])[:, :, :]
                for t in range(2):
                    i = 2 * order + t
                    nc.vector.bn_stats(stats[:, i, :], source[:, t, :]).then_inc(r.now["stats"], 1)
                for t in range(2):
                    i = 2 * order + t
                    dve.wait_ge(r.now["stats"], i + 1)
                    nc.vector.bn_aggr(mean_var[:, i, :], stats[:, i, :]).then_inc(r.now["moments"], 1)

            def negative_mean(r, order):
                at = slice(2 * order, 2 * order + 2)
                dve.wait_ge(r.now["rstd"], order + 1)
                nc.vector.scalar_tensor_tensor(out=neg_mean[:, at], in0=mean_var[:, at, 0], scalar=-1.0,
                                               in1=rstd[:, at], op0=ALU.mult, op1=ALU.mult).then_inc(r.now["negmean"], 1)

            def h_hi(r, order):
                dve.wait_ge(r.now["relu"], order + 1)
                if r.known("side", order):
                    turned = r.plan.fill("h", r.plan.norms[order - 1]) if order else 0
                    dve.wait_ge(*r.count("side", turned))
                nc.vector.tensor_copy(h16[:, 0, :, :], h32[:, :, :]).then_inc(r.now["hhi"], 1)

            def qk_hi(r, n, which):
                dve.wait_ge(r.now["qk32"], 2 * n + which + 1)
                if r.known("qkept", n):
                    dve.wait_ge(*r.count(("qkept", "kkept")[which], 16 * n))
                nc.vector.tensor_copy(qk16[:, which, 0, :, :], qk32[:, :, :]).then_inc(r.now["qkhi"], 1)

            def first_residual(r, m):
                bank = side_bank(r.plan, "o", m)
                order = r.plan.tails.index(m)
                norm = r.plan.norms.index(("tail", m))
                dve.wait_ge(r.now["side"], r.plan.fill("o", m))
                dve.wait_ge(r.now["xbias"], order + 1)
                if r.known("base", order) and not (order and r is REST):
                    last = r.plan.norms.index(("tail", r.plan.tails[order - 1])) + 1 if order else 0
                    dve.wait_ge(*r.count("relu", last))
                    dve.wait_ge(*r.count("base", 2 * order))
                nc.vector.scalar_tensor_tensor(
                    out=x1_of(r.plan, m)[:, :, :], in0=bank[:, :].rearrange("p (t c) -> p t c", t=2),
                    scalar=1.0 / W_SCALE, in1=x_in[:, norm % 2, :, :], op0=ALU.mult, op1=ALU.add).then_inc(r.now["x1done"], 1)
                dve.wait_ge(r.now["x1done"], order + 1)

            def message_hi(r, tile):
                dve.wait_ge(r.now["m32"], r.plan.messages(tile))
                copy = m32[:, r.plan.copies.index(("m", tile)) % 2, :]
                nc.vector.tensor_copy(msg16[:, tile, 0, :], copy[:, D:2 * D]).then_inc(r.now["msghi"], 1)

            def side(r, s):
                for k in r.plan.blocks_at(s, 1):
                    normalise(r, k)
                    if not r.plan.own:
                        o_lo(dve, r, k)
                for order, job in r.plan.norms_at(s, -7):
                    statistics(r, order, job)
                for order, _ in r.plan.norms_at(s, -5):
                    negative_mean(r, order)
                for order, _ in r.plan.norms_at(s, r.plan.split):
                    h_hi(r, order)
                    if not r.plan.own:
                        h_lo(dve, r, order)
                for n in r.plan.piece_at(s, "q", 1):
                    qk_hi(r, n, 0)
                    if not r.plan.own:
                        qk_lo(dve, r, n, 0)
                for n in r.plan.piece_at(s, "k", 1):
                    qk_hi(r, n, 1)
                    if not r.plan.own:
                        qk_lo(dve, r, n, 1)
                for tile in r.plan.piece_at(s, "m", 1):
                    message_hi(r, tile)
                    if not r.plan.own:
                        message_lo(dve, r, tile)
                        own_terms(dve, r, tile)
                for m in r.plan.piece_at(s, "o"):
                    first_residual(r, m)

            def a_round(r):
                for s in range(r.plan.steps):
                    if r.plan.own:
                        mask_scores(r, s)
                    if r is SETUP and s == WEIGHTS:
                        weight_lo()
                    if r is SETUP and s - 1 in ADJ:
                        adj_masks(ADJ.index(s - 1))
                    for k in r.plan.sums_at(s):
                        inverse_sums(r, k)
                    for u in r.plan.unit_at(s, 2):
                        copy_half(r, u)
                    side(r, s)
                    if r.was and s == ARRIVE:
                        arrive(dve)
                if r.was:
                    let_go(dve, "dve")

            dve.wait_ge(s_ident, 16)
            nc.vector.tensor_copy(ident16[:, :], ident32[:, :]).then_inc(s_id16, 1)
            a_round(SETUP)
            a_round(FIRST)
            with dve.Fori(0, (B - 2) // 2):
                a_round(MIDDLE[1])
                a_round(MIDDLE[0])
            a_round(LAST)
            a_round(REST)

        @block.gpsimd
        def _(pool):
            def inverse_deviation(r, order):
                at = slice(2 * order, 2 * order + 2)
                pool.wait_ge(r.now["moments"], 2 * order + 2)
                nc.gpsimd.tensor_scalar(var_eps[:, at], mean_var[:, at, 1], 1.0, EPS, ALU.mult,
                                        ALU.add).then_inc(r.now["vareps"], 1)
                pool.wait_ge(r.now["vareps"], order + 1)
                nc.gpsimd.tensor_tensor(rstd[:, at], var_eps[:, at], minus_half[:, :], ALU.pow).then_inc(r.now["rstd"], 1)

            def repeat_inverse(r, k):
                pool.wait_ge(*r.count("invunit", k + 1))
                if r.known("invtp", k):
                    pool.wait_ge(*r.count("invtp", k))
                units = inv_unit[:, :].rearrange("p (h q) -> p q h", q=2)
                nc.gpsimd.tensor_copy(inv_sum[:, :, :, :],
                                      units[:, :, :, None].to_broadcast([P, 2, GH, DH])).then_inc(r.of(k)["inv"], 1)

            def v_bias(r, n):
                pool.wait_ge(r.now["v32"], n + 1)
                if r is SETUP and n == 0:
                    pool.wait_ge(s_const, 16 * 4)
                for t in range(2):
                    op = nc.gpsimd.tensor_tensor(v32[:, t, :], v32[:, t, :], bias_v[:, :], ALU.add)
                op.then_inc(r.now["v"], 1)

            def x_bias(r, m):
                norm = r.plan.norms.index(("tail", m))
                pool.wait_ge(r.now[("x0", "x1")[norm % 2]], 16 * (norm // 2 + 1))
                for t in range(2):
                    op = nc.gpsimd.tensor_tensor(x_in[:, norm % 2, t, :], x_in[:, norm % 2, t, :], bias_o[:, :],
                                                 ALU.add)
                op.then_inc(r.now["xbias"], 1)

            def result(r, i):
                pool.wait_ge(r.now["sum32"], i + 1)
                if i == 0:
                    pool.wait_ge(r.now["base"], r.plan.messages(NT - 1))
                nc.gpsimd.tensor_tensor(base[:, i, :], base[:, i, :], m32[:, r.plan.copies.index(("a", i)) % 2, 0:D],
                                        ALU.add).then_inc(r.now["result"], 1)

            def side(r, s):
                if r.plan.own:
                    for k in r.plan.blocks_at(s, 1):
                        o_lo(pool, r, k)
                for m in r.plan.piece_at(s, "o", -1):
                    x_bias(r, m)
                for order, _ in r.plan.norms_at(s, -7):
                    inverse_deviation(r, order)
                if r.plan.own:
                    for order, _ in r.plan.norms_at(s, r.plan.split):
                        h_lo(pool, r, order)
                    for n in r.plan.piece_at(s, "q", 1):
                        qk_lo(pool, r, n, 0)
                for n in r.plan.piece_at(s, "v", 1):
                    v_bias(r, n)
                if r.plan.own:
                    for n in r.plan.piece_at(s, "k", 1):
                        qk_lo(pool, r, n, 1)
                    for tile in r.plan.piece_at(s, "m", 1):
                        message_lo(pool, r, tile)
                        own_terms(pool, r, tile)
                for i in r.plan.piece_at(s, "a", 1):
                    result(r, i)

            def clear(semaphores, reached):
                pool.wait_ge(s_arrive, 4)
                for name, value in reached.items():
                    pool.wait_ge(semaphores[name], value)
                for name in reached:
                    pool.sem_clear(semaphores[name])
                pool.sem_clear(s_arrive)
                for s in go.values():
                    pool.sem_inc(s, 1)

            def a_round(r):
                for s in range(r.plan.steps):
                    side(r, s)
                    for k in r.plan.sums_at(s):
                        repeat_inverse(r, k)
                    if r.was and s == CLEAR:
                        clear(r.was, r.before.totals())

            def make_up(r, plan):
                for name, value in plan.totals().items():
                    short = r.plan.totals().get(name, 0)
                    if value > short:
                        if short:
                            pool.wait_ge(r.now[name], short)
                        pool.sem_inc(r.now[name], value - short)

            nc.gpsimd.memset(minus_half[:, :], -0.5).then_inc(s_half, 1)
            pool.wait_ge(s_half, 1)
            a_round(SETUP)
            a_round(FIRST)
            make_up(FIRST, middle)
            with pool.Fori(0, (B - 2) // 2):
                a_round(MIDDLE[1])
                a_round(MIDDLE[0])
            a_round(LAST)
            a_round(REST)
            for name, value in REST.plan.totals().items():
                pool.wait_ge(REST.now[name], value)


def kernel(x, adj, L0_gnn_Wq, L0_gnn_bq, L0_gnn_Wk, L0_gnn_bk, L0_gnn_Wv, L0_gnn_bv, L0_gnn_Wo, L0_gnn_bo,
           L1_gnn_W, L1_gnn_b):
    import numpy as np
    import concourse.bacc as bacc
    from concourse.bass_utils import run_bass_kernel_spmd

    W = np.asarray(L1_gnn_W)
    w_t = np.concatenate([np.asarray(w).T for w in (L0_gnn_Wq, L0_gnn_Wk, L0_gnn_Wv, L0_gnn_Wo, W[:, :D], W[:, D:])],
                         axis=1)
    b_qk = np.stack([np.asarray(L0_gnn_bq).reshape(KC, P), np.asarray(L0_gnn_bk).reshape(KC, P)]).transpose(2, 0, 1)
    arrays = {
        "in_x": x, "in_adj": adj, "in_w_t": w_t, "in_b_qk": b_qk,
        "in_b_v": np.asarray(L0_gnn_bv)[None], "in_b_o": np.asarray(L0_gnn_bo)[None],
        "in_b_msg": np.asarray(L1_gnn_b)[None], "in_ident": np.eye(P, dtype=np.float32),
    }
    arrays = {n: np.ascontiguousarray(a) for n, a in arrays.items()}
    nc = bacc.Bacc("TRN2", target_bir_lowering=False, num_devices=1)
    args = [nc.dram_tensor(n, a.shape, mybir.dt.from_np(a.dtype), kind="ExternalInput").ap()
            for n, a in arrays.items()]
    qk_dram = nc.dram_tensor("qk_next", (2, 2, KC, P, N), F16, kind="Internal").ap()
    v_dram = nc.dram_tensor("v_next", (N, D), F32, kind="Internal").ap()
    result = nc.dram_tensor("out", (B, N, D), F32, kind="ExternalOutput").ap()
    gnn_kernel(nc, *args, qk_dram, v_dram, result)
    r = run_bass_kernel_spmd(nc, [arrays], core_ids=[0])
    return r.results[0]["out"]
```
